# Optimizing a Trainium2 kernel written in Bass

```python
import numpy as np
import jax
import jax.numpy as jnp

def _softmax(x, axis=-1):
    return jax.nn.softmax(x, axis=axis)

def _gelu(x):
    return jax.nn.gelu(x, approximate=True)

def _silu(x):
    return jax.nn.silu(x)

def _sigmoid(x):
    return jax.nn.sigmoid(x)

def _layernorm(x, axis=-1, eps=1e-05):
    m = jnp.mean(x, axis=axis, keepdims=True)
    v = jnp.var(x, axis=axis, keepdims=True)
    return (x - m) / jnp.sqrt(v + eps)

def _scatter_add(tgt, idx, src, axis=0):
    return tgt.at[idx].add(src)

def _segment_sum(src, seg, n):
    return jax.ops.segment_sum(src, seg, n)
kernel_name = 'mk_gnn_preln_d1_gnn_r8_d11a39'

def setup_inputs(seed: int=0):
    np.random.seed(seed)
    _w = jnp.asarray

    def _rec_inputs():
        import jax
        import jax.numpy as jnp
        _gk = jax.random.key(seed)
        x = -0.0005121 + 1.001 * jax.random.normal(jax.random.fold_in(_gk, 1), (6250, 64), jnp.float32)
        src = jax.random.randint(jax.random.fold_in(_gk, 2), (200000,), 0, 6250, jnp.int32)
        dst = jax.random.randint(jax.random.fold_in(_gk, 3), (200000,), 0, 6250, jnp.int32)
        _o = jnp.argsort(dst, stable=True)
        src = src[_o]
        dst = dst[_o]
        edge_type_16 = jax.random.randint(jax.random.fold_in(_gk, 12), (200000,), 0, 16, jnp.int32)
        return (x, src, dst, edge_type_16)
    x, src, dst, edge_type_16 = _rec_inputs()

    def _L0_gnn_setup():
        import jax, jax.numpy as jnp
        import numpy as np
        N_NODES = 6250
        N_EDGES = 100000
        D_IN = 64
        D_OUT = 64
        NUM_RELS = 16
        key = jax.random.key(seed)
        k1, k2, k3, k4, k5 = jax.random.split(key, 5)
        feat = jax.random.normal(k1, (N_NODES, D_IN), dtype=jnp.float32)
        weight = jax.random.normal(k2, (NUM_RELS, D_IN, D_OUT), dtype=jnp.float32) * 0.05
        src = jax.random.randint(k3, (N_EDGES,), 0, N_NODES, dtype=jnp.int32)
        dst = jax.random.randint(k4, (N_EDGES,), 0, N_NODES, dtype=jnp.int32)
        etypes = jax.random.randint(k5, (N_EDGES,), 0, NUM_RELS, dtype=jnp.int32)
        return {'feat': feat, 'weight': weight, 'src': src, 'dst': dst, 'etypes': etypes}
    _L0_gnn_all = _L0_gnn_setup()
    _L0_gnn_in = {k: v for k, v in _L0_gnn_all.items() if k in ('weight',)}
    del _L0_gnn_all
    return {'x': x, 'src': src, 'dst': dst, 'edge_type_16': edge_type_16, 'L0_gnn_weight': _L0_gnn_in['weight']}

def reference(x, src, dst, edge_type_16, L0_gnn_weight):
    import jax
    import jax.numpy as jnp

    def _L0_gnn_ref(feat, weight, src, dst, etypes):
        import jax, jax.numpy as jnp
        import numpy as np
        N_NODES = 6250
        N_EDGES = 100000
        D_IN = 64
        D_OUT = 64
        NUM_RELS = 16
        num_rels = weight.shape[0]
        h_src = feat[src]
        msg = jnp.zeros((h_src.shape[0], weight.shape[2]), dtype=feat.dtype)
        for r in range(num_rels):
            mask = etypes == r
            msg = msg + h_src * mask[:, None].astype(feat.dtype) @ weight[r]
        out = jax.ops.segment_sum(msg, dst, num_segments=feat.shape[0])
        return out
    h = jnp.maximum(_layernorm(x, axis=-1), 0.0)
    x = x + _L0_gnn_ref(h, L0_gnn_weight, src, dst, edge_type_16)
    return x

_drawn_inputs = setup_inputs


def setup_inputs(seed=0):
    import zlib

    import numpy as np

    out = dict(_drawn_inputs(seed))
    spreads = {}
    factors = {}
    for name, (base, spread) in spreads.items():
        noise = np.random.default_rng([zlib.crc32(name.encode()), seed]).standard_normal(out[name].shape)
        drawn = base * np.exp(spread * noise) if base else spread * noise
        out[name] = jnp.asarray(drawn.astype(out[name].dtype))
    for name, factor in factors.items():
        out[name] = (out[name] * factor).astype(out[name].dtype)
    return out
```

```python
from contextlib import ExitStack

import numpy as np
import concourse.bass as bass
import concourse.mybir as mybir

F32 = mybir.dt.float32
I32 = mybir.dt.int32
ALU = mybir.AluOpType
ACT = mybir.ActivationFunctionType
AX = mybir.AxisListType.X
P = 128
EPS = 1e-5


def wait(eng, sem, value):
    if not isinstance(value, int) or value > 0:
        eng.wait_ge(sem, value)


def hold(eng, sem, value):
    wait(eng, sem, value)
    if not isinstance(value, int):
        eng.nop(nofuse=True)


class Counted:

    def __init__(self, sem):
        self.sem, self.n = sem, 0

    def inc(self, ins):
        self.n += 1
        ins.then_inc(self.sem, 1)
        return self.n

    def then_wait(self, eng, ins):
        eng.wait_ge(self.sem, self.inc(ins))


def gnn_program(nc, x, src, dst, etype, weight, out):
    N, D = x.shape
    E = src.shape[0]
    R = weight.shape[0]
    NT = -(-N // P)
    NREM = N - (NT - 1) * P
    GT = 7
    NG = NT // GT
    assert NG * GT == NT
    HALF = R * D // 2
    ST = 8
    WIN = 64
    ET = -(-E // P)
    EB = -(-ET // P)
    ETFULL = E // P
    EREM = E - ETFULL * P
    NS = ET // ST
    TAIL = ET - NS * ST
    NSB = P // ST
    assert TAIL and EREM and NS % 2 == 1 and EB % 2 == 1

    table = nc.dram_tensor("table", [NT * P * R, D], F32).ap()

    ctx = ExitStack()
    sb = lambda name, shape, dt=F32: ctx.enter_context(nc.sbuf_tensor(name, shape, dt))
    sem = lambda name: ctx.enter_context(nc.semaphore(name))
    with ctx:
        x_sb = sb("x_sb", [P, NT, D])
        w_sb = sb("w_sb", [D, R, D])
        ident = sb("ident", [P, P])
        iota_nodes = sb("iota_nodes", [P, NT * P])
        nat_src = sb("nat_src", [P, EB, P], I32)
        nat_typ = sb("nat_typ", [P, EB, P], I32)
        nat_dst = sb("nat_dst", [P, EB, P], I32)
        tile_min = sb("tile_min", [P, EB])
        tile_max = sb("tile_max", [P, EB])
        super_min = sb("super_min", [EB, NSB])
        super_max = sb("super_max", [EB, NSB])
        super_base = sb("super_base", [EB, NSB], I32)
        base_spread = sb("base_spread", [EB, P])
        base_nat = sb("base_nat", [P, EB])
        base_row = sb("base_row", [1, EB * NSB], I32)
        span = sb("span", [EB, 1])
        span_all = sb("span_all", [1, 1], I32)
        stage = sb("stage", [P, 2, 3, P])
        row_idx = sb("row_idx", [P, EB * P], I32)
        dst_abs = sb("dst_abs", [P, EB * P])
        dst_rel = sb("dst_rel", [P, EB * P])
        stat = sb("stat", [P, 5, GT])
        centred = sb("centred", [P, GT, D])
        squares = sb("squares", [P, GT, D])
        h_sb = sb("h_sb", [P, GT, D])
        hT = sb("hT", [D, GT, P])
        t_sb = sb("t_sb", [P, GT, R * D])
        msg = sb("msg", [P, 2, ST, D])
        idx_slot = sb("idx_slot", [P, 2, ST], I32)
        onehot = sb("onehot", [P, ST * P])
        accT = sb("accT", [D, NT * P + WIN])
        acc_stage = sb("acc_stage", [D, 2, GT * P])
        res = sb("res", [P, 2, GT, D])
        ps = [ctx.enter_context(nc.psum_tensor(f"ps{i}", [P, 512], F32)) for i in range(8)]

        s_pad, s_id, s_iota, s_acc0 = sem("s_pad"), sem("s_id"), sem("s_iota"), sem("s_acc0")
        s_x = [sem(f"s_x{i}") for i in range(3)]
        s_w = sem("s_w")
        s_edges = [sem(f"s_edges{i}") for i in range(3)]
        s_base_row = sem("s_base_row")
        s_prep = Counted(sem("s_prep"))
        s_prep_pe = Counted(sem("s_prep_pe"))
        s_stage, s_stT = sem("s_stage"), sem("s_stT")
        s_stE = [sem("s_stE_act"), sem("s_stE_dve")]
        s_var = sem("s_var")
        s_ln, s_sq, s_rt, s_h = sem("s_ln"), sem("s_sq"), sem("s_rt"), sem("s_h")
        s_lnc = sem("s_lnc")
        s_hp, s_hT, s_mmT = sem("s_hp"), sem("s_hT"), sem("s_mmT")
        s_ev = [sem("s_evA"), sem("s_evV")]
        s_tw = [sem(f"s_tw{k}") for k in range(GT)]
        s_g = [[sem(f"s_g{b}_{k}") for k in range(ST)] for b in range(2)]
        s_oh, s_mm, s_add = sem("s_oh"), sem("s_mm"), sem("s_add")
        s_goh, s_gmm, s_gadd = sem("s_goh"), sem("s_gmm"), sem("s_gadd")
        s_ix, s_gix = sem("s_ix"), sem("s_gix")
        s_as, s_oT, s_res = sem("s_as"), sem("s_oT"), sem("s_res")
        s_out = [sem(f"s_out{i}") for i in range(2)]

        tile_rows = lambda k, tiles: EREM if tiles == TAIL and k == TAIL - 1 else P

        block = ctx.enter_context(nc.Block())

        @block.sync
        def _(sp):
            wait(sp, s_pad, 4)
            blocks = E // (P * P)
            rest = E - blocks * P * P
            for arr, nat, s in ((dst, nat_dst, s_edges[0]), (src, nat_src, s_edges[1]), (etype, nat_typ, s_edges[2])):
                sp.dma_start(nat[:, 0:blocks, :],
                             arr[0:blocks * P * P].rearrange("(b q p) -> q b p", q=P, p=P)).then_inc(s, 16)
                sp.dma_start(nat[0:rest // P, blocks, :],
                             arr[blocks * P * P:ETFULL * P].rearrange("(q p) -> q p", p=P)).then_inc(s, 16)
                sp.dma_start(nat[rest // P:rest // P + 1, blocks, 0:EREM],
                             arr[ETFULL * P:E].rearrange("(q p) -> q p", q=1)).then_inc(s, 16)
            q = rest // P
            sp.dma_start(nat_dst[q:q + 1, blocks, EREM:P],
                         dst[E - (P - EREM):E].rearrange("(q p) -> q p", q=1)).then_inc(s_edges[0], 16)
            for r in range(q + 1, -(-(q + 1) // ST) * ST):
                sp.dma_start(nat_dst[r:r + 1, blocks, :],
                             dst[E - P:E].rearrange("(q p) -> q p", q=1)).then_inc(s_edges[0], 16)

            def store_tile(g, k):
                wait(sp, s_ev[0], g * GT + k + 1)
                wait(sp, s_ev[1], g * GT + k + 1)
                rows = table.rearrange("(t p r) d -> t p (r d)", p=P, r=R)[bass.ds(g * GT + k, 1)]
                sp.dma_start(rows.rearrange("o p c -> (o p) c"),
                             t_sb[:, k, :]).then_inc(s_tw[k], 16)

            wait(sp, s_prep.sem, PREP["base"])
            sp.dma_start(base_row[:, :].rearrange("o (b s) -> o b s", b=EB), super_base[:, :]).then_inc(s_base_row, 16)
            with sp.Fori(0, NG) as g:
                for k in range(GT):
                    store_tile(g, k)

            def store_out(g, slot):
                wait(sp, s_res, g + 1)
                if isinstance(g, int) and g == NG - 1:
                    full = GT - 1
                    t0 = g * GT
                    sp.dma_start(out[t0 * P:(NT - 1) * P, :].rearrange("(t p) d -> p t d", p=P),
                                 res[:, slot, 0:full, :]).then_inc(s_out[slot], 16)
                    a = NREM // 16 * 16
                    sp.dma_start(out[(NT - 1) * P:(NT - 1) * P + a, :], res[0:a, slot, full, :]).then_inc(s_out[slot], 16)
                    sp.dma_start(out[(NT - 1) * P + a:N, :], res[a:NREM, slot, full, :]).then_inc(s_out[slot], 16)
                else:
                    sp.dma_start(out[bass.ds(g * (GT * P), GT * P), :].rearrange("(t p) d -> p t d", p=P),
                                 res[:, slot, :, :]).then_inc(s_out[slot], 16)

            with sp.Fori(0, NG // 2) as i:
                for b in range(2):
                    store_out(2 * i + b, b)
            store_out(NG - 1, 0)
            wait(sp, s_out[0], 16 * (NG // 2 + 3))
            wait(sp, s_out[1], 16 * (NG // 2))

        @block.gpsimd
        def _(pool):
            blocks = E // (P * P)
            pool.memset(x_sb[:, NT - 1, :], 0.0).then_inc(s_pad, 1)
            for nat in (nat_dst, nat_src, nat_typ):
                pool.memset(nat[:, blocks, :], 0).then_inc(s_pad, 1)
            pool.memset(ident[:, :], 0.0).then_inc(s_id, 1)
            wait(pool, s_id, 1)
            pool.affine_select(out=ident[:, :], in_=ident[:, :], compare_op=ALU.not_equal, fill=1.0, base=0,
                               pattern=[[-1, P]], channel_multiplier=1).then_inc(s_id, 1)
            pool.iota(iota_nodes[:, :], [[1, NT * P]], base=0, channel_multiplier=0,
                      allow_small_or_imprecise_dtypes=True).then_inc(s_iota, 1)

            def gather(s, b, tiles):
                for k in range(tiles):
                    n = tile_rows(k, tiles)
                    pool.indirect_dma_start(
                        out=msg[0:n, b, k, :], out_offset=None, in_=table,
                        in_offset=bass.IndirectOffsetOnAxis(ap=idx_slot[0:n, b, k:k + 1], axis=0),
                    ).then_inc(s_g[b][k], 16)

            def gather_fast(s, b, tiles=ST):
                hold(pool, s_ix, s + 1)
                gather(s, b, tiles)

            def gather_general(s, tiles=ST):
                hold(pool, s_gix, s + 1)
                gather(s, 0, tiles)

            wait(pool, s_stE[1], EB)
            for k in range(GT):
                wait(pool, s_tw[k], 16 * NG)
            wait(pool, s_prep.sem, PREP["flag"])
            spread = pool.value_load(span_all[0:1, 0:1], min_val=0, max_val=N)
            with pool.If(spread < WIN):
                gather_fast(0, 0)
                gather_fast(1, 1)
                with pool.Fori(1, NS // 2) as i:
                    gather_fast(2 * i, 0)
                    gather_fast(2 * i + 1, 1)
                gather_fast(NS - 1, 0)
                gather_fast(NS, 1, TAIL)
            with pool.Else():
                with pool.Fori(0, NS) as s:
                    gather_general(s)
                gather_general(NS, TAIL)

        @block.scalar
        def _(act):
            for a, b, s in ((0, NT // 2, 0), (NT // 2, NT - 1, 1)):
                act.dma_start(x_sb[:, a:b, :], x[a * P:b * P, :].rearrange("(t p) d -> p t d", p=P)).then_inc(s_x[s], 16)
            a = NREM // 16 * 16
            wait(act, s_pad, 4)
            act.dma_start(x_sb[0:a, NT - 1, :], x[(NT - 1) * P:(NT - 1) * P + a, :]).then_inc(s_x[2], 16)
            act.dma_start(x_sb[a:NREM, NT - 1, :], x[(NT - 1) * P + a:N, :]).then_inc(s_x[2], 16)
            act.dma_start(w_sb[:, :, :], weight.rearrange("r i o -> i r o")).then_inc(s_w, 16)

            def evac_edges(b, slot):
                wait(act, s_stT, b + 1)
                act.copy(dst_abs[:, bass.ts(b, P)], ps[4 + slot][:, 0:P])
                act.copy(dst_rel[:, bass.ts(b, P)], ps[4 + slot][:, P:2 * P]).then_inc(s_stE[0], 1)

            with act.Fori(0, EB // 2) as i:
                for b in range(2):
                    evac_edges(2 * i + b, b)
            evac_edges(EB - 1, 0)

            def group(g):
                wait(act, s_ln, g + 1)
                act.activation(squares[:, :, :], centred[:, :, :], ACT.Square).then_inc(s_sq, 1)
                wait(act, s_var, g + 1)
                act.activation(stat[:, 3, :], stat[:, 2, :], ACT.Sqrt).then_inc(s_rt, 1)
                for part, (a, b) in enumerate(((0, 4), (4, GT))):
                    wait(act, s_hp, 2 * g + part + 1)
                    if part == 0:
                        wait(act, s_mmT, 2 * GT * g)
                    act.copy(hT[:, a:b, :].rearrange("d t p -> d (t p)"), ps[part][0:D, 0:(b - a) * P]).then_inc(s_hT, 1)
                for k in range(GT):
                    wait(act, s_mmT, 2 * (g * GT + k) + 1)
                    wait(act, s_tw[k], 16 * g)
                    act.copy(t_sb[:, k, 0:HALF], ps[2 + k % 2][:, 0:HALF]).then_inc(s_ev[0], 1)

            group(0)
            with act.Fori(1, NG) as g:
                group(g)

            def stage_acc(g, slot):
                wait(act, s_oT, g - 1)
                act.copy(acc_stage[:, slot, :], accT[:, bass.ts(g, GT * P)]).then_inc(s_as, 1)

            wait(act, s_acc0, 2)
            stage_acc(0, 0)
            stage_acc(1, 1)
            with act.Fori(1, NG // 2) as i:
                for b in range(2):
                    stage_acc(2 * i + b, b)
            stage_acc(NG - 1, 0)

        @block.vector
        def _(dve):
            dve.memset(accT[:, :], 0.0).then_inc(s_acc0, 1)
            c = s_prep
            n_dst_dmas = 3 + 1 + PREP["pad_rows"]
            wait(dve, s_edges[0], 16 * n_dst_dmas)
            c.inc(dve.tensor_reduce(tile_min[:, :], nat_dst[:, :, :], AX, ALU.min))
            c.inc(dve.tensor_reduce(tile_max[:, :], nat_dst[:, :, :], AX, ALU.max))
            PREP["tile"] = c.n
            wait(dve, s_prep_pe.sem, 2)
            v = lambda t: t.rearrange("b (s t) -> b s t", t=ST)
            c.inc(dve.tensor_reduce(super_min[:, :], v(ps[0][0:EB, 0:P]), AX, ALU.min))
            c.then_wait(dve, dve.tensor_reduce(super_max[:, :], v(ps[1][0:EB, 0:P]), AX, ALU.max))
            c.inc(dve.tensor_copy(super_base[:, :], super_min[:, :]))
            assert c.n == PREP["base"]
            c.inc(dve.tensor_copy(v(base_spread[:, :]), super_min[:, :].rearrange("b (s o) -> b s o", o=1).to_broadcast([EB, NSB, ST])))
            c.then_wait(dve, dve.tensor_tensor(super_max[:, :], super_max[:, :], super_min[:, :], ALU.subtract))
            c.inc(dve.tensor_reduce(span[:, :], super_max[:, :], AX, ALU.max))
            assert c.n == PREP["span"]
            wait(dve, s_prep_pe.sem, 4)
            c.then_wait(dve, dve.tensor_copy(base_nat[:, :], ps[2][:, 0:EB]))
            c.inc(dve.tensor_reduce(span_all[:, :], ps[3][0:1, 0:EB], AX, ALU.max))
            assert c.n == PREP["flag"]
            wait(dve, s_edges[1], 48)
            wait(dve, s_edges[2], 48)

            def stage_block(b, slot):
                wait(dve, s_stT, b - 1)
                one = lambda t: t[:, bass.ds(b, 1), :].rearrange("q o p -> q (o p)")
                dve.scalar_tensor_tensor(stage[:, slot, 0, :], one(nat_src), float(R), one(nat_typ), ALU.mult, ALU.add)
                dve.tensor_copy(stage[:, slot, 1, :], one(nat_dst))
                dve.tensor_scalar(stage[:, slot, 2, :], one(nat_dst), base_nat[:, bass.ds(b, 1)], None, ALU.subtract).then_inc(s_stage, 1)

            def evac_block(b, slot):
                wait(dve, s_stT, b + 1)
                dve.tensor_copy(row_idx[:, bass.ts(b, P)], ps[6 + slot][:, 0:P]).then_inc(s_stE[1], 1)

            stage_block(0, 0)
            stage_block(1, 1)
            evac_block(0, 0)
            with dve.Fori(1, EB // 2) as i:
                stage_block(2 * i, 0)
                evac_block(2 * i - 1, 1)
                stage_block(2 * i + 1, 1)
                evac_block(2 * i, 0)
            stage_block(EB - 1, 0)
            evac_block(EB - 2, 1)
            evac_block(EB - 1, 0)

            def spread_over(t):
                return t.rearrange("p (t o) -> p t o", o=1).to_broadcast([P, GT, D])

            def group(g):
                xg = x_sb[:, bass.ts(g, GT), :]
                steps = 5
                at = [g * steps]

                def chained(ins):
                    at[0] = at[0] + 1
                    ins.then_inc(s_lnc, 1)
                    wait(dve, s_lnc, at[0])

                chained(dve.tensor_reduce(stat[:, 0, :], xg, AX, ALU.add))
                chained(dve.tensor_scalar(stat[:, 1, :], stat[:, 0, :], 1.0 / D, None, ALU.mult))
                wait(dve, s_h, g)
                dve.tensor_tensor(centred[:, :, :], xg, spread_over(stat[:, 1, :]), ALU.subtract).then_inc(s_ln, 1)
                wait(dve, s_sq, g + 1)
                chained(dve.tensor_reduce(stat[:, 4, :], squares[:, :, :], AX, ALU.add))
                dve.tensor_scalar(stat[:, 2, :], stat[:, 4, :], 1.0 / D, EPS, ALU.mult, ALU.add).then_inc(s_var, 1)
                wait(dve, s_rt, g + 1)
                chained(dve.reciprocal(stat[:, 4, :], stat[:, 3, :]))
                wait(dve, s_hp, 2 * g)
                dve.scalar_tensor_tensor(h_sb[:, :, :], centred[:, :, :], 0.0, spread_over(stat[:, 4, :]), ALU.max, ALU.mult).then_inc(s_h, 1)
                chained(dve.memset(stat[:, 0, 0:1], 0.0))
                for k in range(GT):
                    wait(dve, s_mmT, 2 * (g * GT + k) + 2)
                    wait(dve, s_tw[k], 16 * g)
                    dve.tensor_copy(t_sb[:, k, HALF:], ps[4 + k % 2][:, 0:HALF]).then_inc(s_ev[1], 1)

            for s in s_x[0:2]:
                wait(dve, s, 16)
            wait(dve, s_x[2], 32)
            group(0)
            with dve.Fori(1, NG) as g:
                group(g)

            wait(dve, s_iota, 1)
            wait(dve, s_base_row, 16)
            spread = dve.value_load(span_all[0:1, 0:1], min_val=0, max_val=N)

            def compare(out_ap, nodes_ap, keys_ap, width):
                return dve.tensor_tensor(out_ap, nodes_ap.rearrange("p (o w) -> p o w", o=1).to_broadcast([P, ST, width]),
                                         keys_ap.rearrange("p (t o) -> p t o", o=1).to_broadcast([P, ST, width]), ALU.is_equal)

            def fast_onehot(s, b):
                wait(dve, s_mm, s - 1)
                dve.tensor_copy(idx_slot[:, b, :], row_idx[:, bass.ts(s, ST)]).then_inc(s_ix, 1)
                oh = onehot[:, b * ST * WIN:(b + 1) * ST * WIN].rearrange("p (t w) -> p t w", w=WIN)
                compare(oh, iota_nodes[:, 0:WIN], dst_rel[:, bass.ts(s, ST)], WIN).then_inc(s_oh, 1)

            def fast_add(s, b):
                base = dve.value_load(base_row[0:1, bass.ds(s, 1)], min_val=0, max_val=N)
                wait(dve, s_add, s)
                wait(dve, s_mm, s + 1)
                here = accT[:, bass.ds(base, WIN)]
                dve.tensor_tensor(here, here, ps[b][0:D, 0:WIN], ALU.add).then_inc(s_add, 1)

            def general_window(s, w):
                u = s * NT + w
                compare(onehot[:, :].rearrange("p (t w) -> p t w", w=P), iota_nodes[:, bass.ts(w, P)],
                        dst_abs[:, bass.ts(s, ST)], P).then_inc(s_goh, 1)
                wait(dve, s_gmm, u + 1)
                here = accT[:, bass.ts(w, P)]
                dve.tensor_tensor(here, here, ps[0][0:D, 0:P], ALU.add).then_inc(s_gadd, 1)
                wait(dve, s_gadd, u + 1)

            with dve.If(spread < WIN):
                fast_onehot(0, 0)
                fast_onehot(1, 1)
                fast_add(0, 0)
                with dve.Fori(1, NS // 2 + 1) as i:
                    fast_onehot(2 * i, 0)
                    fast_add(2 * i - 1, 1)
                    fast_onehot(2 * i + 1, 1)
                    fast_add(2 * i, 0)
                fast_add(NS, 1)
                wait(dve, s_add, NS + 1)
            with dve.Else():
                with dve.Fori(0, NS + 1) as s:
                    dve.tensor_copy(idx_slot[:, 0, :], row_idx[:, bass.ts(s, ST)]).then_inc(s_gix, 1)
                    with dve.Fori(0, NT) as w:
                        general_window(s, w)
            dve.memset(stat[:, 0, 0:1], 0.0).then_inc(s_acc0, 1)

            def finish(g, slot):
                wait(dve, s_oT, g + 1)
                wait(dve, s_out[slot], 16 * (g // 2) if isinstance(g, int) else g * 8 - 8 * slot)
                dve.tensor_tensor(res[:, slot, 0:GT, :], ps[2 + slot][:, 0:GT * D].rearrange("p (t d) -> p t d", d=D),
                                  x_sb[:, bass.ts(g, GT), :], ALU.add).then_inc(s_res, 1)

            finish(0, 0)
            finish(1, 1)
            with dve.Fori(1, NG // 2) as i:
                for b in range(2):
                    wait(dve, s_oT, 2 * i + b + 1)
                    wait(dve, s_out[b], 16 * i)
                    dve.tensor_tensor(res[:, b, :, :], ps[2 + b][:, 0:GT * D].rearrange("p (t d) -> p t d", d=D),
                                      x_sb[:, bass.ts(2 * i + b, GT), :], ALU.add).then_inc(s_res, 1)
            finish(NG - 1, 0)

        @block.tensor
        def _(pe):
            c = s_prep_pe
            wait(pe, s_id, 2)
            wait(pe, s_prep.sem, PREP["tile"])
            c.inc(pe.transpose(ps[0][0:EB, 0:P], tile_min[:, :], ident[:, :]))
            c.inc(pe.transpose(ps[1][0:EB, 0:P], tile_max[:, :], ident[:, :]))
            wait(pe, s_prep.sem, PREP["span"])
            c.inc(pe.transpose(ps[2][:, 0:EB], base_spread[:, :], ident[0:EB, 0:EB]))
            c.inc(pe.transpose(ps[3][0:1, 0:EB], span[:, :], ident[0:EB, 0:EB]))

            def turn_block(b, slot):
                hold(pe, s_stage, b + 1)
                for s in s_stE:
                    hold(pe, s, b - 1)
                for a, to in enumerate((ps[6 + slot][:, 0:P], ps[4 + slot][:, 0:P], ps[4 + slot][:, P:2 * P])):
                    last = pe.transpose(to, stage[:, slot, a, :], ident[:, :])
                last.then_inc(s_stT, 1)

            turn_block(0, 0)
            turn_block(1, 1)
            with pe.Fori(1, EB // 2) as i:
                for b in range(2):
                    turn_block(2 * i + b, b)
            turn_block(EB - 1, 0)

            def group(g):
                hold(pe, s_h, g + 1)
                hold(pe, s_hT, 2 * g)
                for part, (a, b) in enumerate(((0, 4), (4, GT))):
                    for k in range(a, b):
                        last = pe.transpose(ps[part][0:D, (k - a) * P:(k - a + 1) * P], h_sb[:, k, :], ident[:, :])
                    last.then_inc(s_hp, 1)
                for k in range(GT):
                    if k in (0, 4):
                        hold(pe, s_hT, 2 * g + (1 if k == 0 else 2))
                    n = g * GT + k
                    prev = n - 1 if k > 1 else n - 2 if k == 1 else n
                    for half in range(2):
                        wait(pe, s_ev[half], prev)
                        pe.matmul(ps[2 + 2 * half + k % 2][:, 0:HALF], hT[:, k, :],
                                  w_sb[:, half * R // 2:(half + 1) * R // 2, :].rearrange("i r o -> i (r o)"),
                                  start=True, stop=True).then_inc(s_mmT, 1)

            wait(pe, s_w, 16)
            for s in s_stE:
                wait(pe, s, EB)
            group(0)
            with pe.Fori(1, NG) as g:
                group(g)

            wait(pe, s_prep.sem, PREP["flag"])
            spread = pe.value_load(span_all[0:1, 0:1], min_val=0, max_val=N)

            def fast_sum(s, b, tiles=ST):
                wait(pe, s_oh, s + 1)
                wait(pe, s_add, s - 1)
                for k in range(tiles):
                    n = tile_rows(k, tiles)
                    wait(pe, s_g[b][k], 16 * (s // 2 + 1) if isinstance(s, int) else 8 * s + (16 - 8 * b))
                    o = b * ST * WIN + k * WIN
                    last = pe.matmul(ps[b][0:D, 0:WIN], msg[0:n, b, k, :], onehot[0:n, o:o + WIN],
                                     start=(k == 0), stop=(k == tiles - 1))
                last.then_inc(s_mm, 1)

            def general_super(s, tiles=ST):
                for k in range(tiles):
                    hold(pe, s_g[0][k], 16 * (s + 1))
                with pe.Fori(0, NT) as w:
                    u = s * NT + w
                    wait(pe, s_goh, u + 1)
                    for k in range(tiles):
                        n = tile_rows(k, tiles)
                        last = pe.matmul(ps[0][0:D, 0:P], msg[0:n, 0, k, :], onehot[0:n, k * P:(k + 1) * P],
                                         start=(k == 0), stop=(k == tiles - 1))
                    last.then_inc(s_gmm, 1)

            with pe.If(spread < WIN):
                fast_sum(0, 0)
                fast_sum(1, 1)
                with pe.Fori(1, NS // 2) as i:
                    fast_sum(2 * i, 0)
                    fast_sum(2 * i + 1, 1)
                fast_sum(NS - 1, 0)
                fast_sum(NS, 1, TAIL)
            with pe.Else():
                with pe.Fori(0, NS) as s:
                    general_super(s)
                general_super(NS, TAIL)

            def turn_back(g, slot):
                hold(pe, s_as, g + 1)
                hold(pe, s_res, g - 1)
                for k in range(GT):
                    last = pe.transpose(ps[2 + slot][:, k * D:(k + 1) * D], acc_stage[:, slot, k * P:(k + 1) * P],
                                        ident[0:D, 0:D])
                last.then_inc(s_oT, 1)

            turn_back(0, 0)
            turn_back(1, 1)
            with pe.Fori(1, NG // 2) as i:
                for b in range(2):
                    turn_back(2 * i + b, b)
            turn_back(NG - 1, 0)


PREP = {"tile": 2, "base": 5, "span": 8, "flag": 10, "pad_rows": 5}


def kernel(x, src, dst, edge_type_16, L0_gnn_weight):
    from concourse import bacc
    from concourse.bass_utils import run_bass_kernel_spmd

    given = {"x": x, "src": src, "dst": dst, "edge_type": edge_type_16, "weight": L0_gnn_weight}
    arrays = {name: np.ascontiguousarray(a) for name, a in given.items()}
    nc = bacc.Bacc("TRN2", target_bir_lowering=False, num_devices=1)
    aps = [nc.dram_tensor(name, a.shape, mybir.dt.from_np(a.dtype), kind="ExternalInput").ap()
           for name, a in arrays.items()]
    out = nc.dram_tensor("out", arrays["x"].shape, F32, kind="ExternalOutput").ap()
    gnn_program(nc, *aps, out)
    run = run_bass_kernel_spmd(nc, [arrays], core_ids=[0])
    return run.results[0]["out"]
```

```python
from contextlib import ExitStack

import numpy as np
import concourse.bass as bass
import concourse.mybir as mybir

F32 = mybir.dt.float32
BF16 = mybir.dt.bfloat16
I32 = mybir.dt.int32
ALU = mybir.AluOpType
ACT = mybir.ActivationFunctionType
AX = mybir.AxisListType.X
P = 128
EPS = 1e-5
BANK = 512


def wait(eng, sem, value):
    if not isinstance(value, int) or value > 0:
        eng.wait_ge(sem, value)


def hold(eng, sem, value):
    wait(eng, sem, value)
    if not isinstance(value, int):
        eng.nop(nofuse=True)


def spread(t, n):
    return t.rearrange("p (m o) -> p m o", o=1).to_broadcast([t.shape[0], t.shape[1], n])


def gnn_program(nc, x, src, dst, etype, weight, out):
    N, D = x.shape
    E = src.shape[0]
    R = weight.shape[0]
    NT = -(-N // P)
    NREM = N - (NT - 1) * P
    GT = 7
    NG = NT // GT
    NPART = 3
    ROW = NPART * D
    assert NG * GT == NT and 2 * D == P

    ET = -(-E // P)
    ETFULL = E // P
    EREM = E - ETFULL * P
    EB = -(-ET // P)
    EBFULL = E // (P * P)
    RESTQ = ETFULL - EBFULL * P
    ST = 2
    WIN = 16
    COLS = R * WIN
    SB = 8
    BT = SB * ST
    NB = ET // BT
    LT = ET - NB * BT
    LS = -(-LT // ST)
    NSB = P // ST
    RING = 4
    HMB, LOB = BANK // COLS, 2 * BANK // COLS
    assert EREM and LT and NB % 2 == 1 and SB % RING == 0 and RESTQ % ST == 0

    GST = 8
    GS = ET // GST
    GTAIL = ET - GS * GST
    HALF = R * D // 2
    assert HALF == BANK and GTAIL

    parts_dram = nc.dram_tensor("parts_dram", [NT * P, ROW], BF16).ap()
    table = nc.dram_tensor("table", [NT * P * R, D], F32).ap()

    ctx = ExitStack()
    sb = lambda name, shape, dt=F32: ctx.enter_context(nc.sbuf_tensor(name, shape, dt))
    sem = lambda name: ctx.enter_context(nc.semaphore(name))
    with ctx:
        x_sb = sb("x_sb", [P, NT, D])
        h_sb = sb("h_sb", [P, NT, D])
        w_hm = sb("w_hm", [P, R, D])
        w_lo = sb("w_lo", [P, R // 2, D])
        ident = sb("ident", [P, P])
        nat_src = sb("nat_src", [P, EB, P], I32)
        nat_typ = sb("nat_typ", [P, EB, P], I32)
        nat_dst = sb("nat_dst", [P, EB, P], I32)
        nat_a = sb("nat_a", [P, EB, P])
        nat_b = sb("nat_b", [P, EB, P])
        row_idx = sb("row_idx", [P, EB * P], I32)
        key = sb("key", [P, EB * P])
        tile_min = sb("tile_min", [P, EB])
        tile_max = sb("tile_max", [P, EB])
        super_min = sb("super_min", [EB, NSB])
        super_max = sb("super_max", [EB, NSB])
        super_base = sb("super_base", [EB, NSB], I32)
        super_span = sb("super_span", [EB, NSB])
        base_spread = sb("base_spread", [EB, P])
        base_nat = sb("base_nat", [P, EB])
        base_row = sb("base_row", [1, EB * NSB], I32)
        span = sb("span", [EB, 1])
        span_all = sb("span_all", [1, 1], I32)
        stat_sum, stat_mean, stat_sq, stat_var, stat_std, stat_rstd = (
            sb(f"stat{i}", [P, NT]) for i in range(6))
        msg = sb("msg", [P, 2, BT, ROW], BF16)
        idx_slot = sb("idx_slot", [P, 2, BT], I32)
        key_slot = sb("key_slot", [P, 2, BT])
        onehot = sb("onehot", [P, RING * ST, COLS], BF16)
        accT = sb("accT", [D, NT * P + WIN])
        big = sb("big", [P, GT * R * D])
        centred = big[:, 0:NT * D].rearrange("p (t d) -> p t d", d=D)
        squares = big[:, NT * D:2 * NT * D].rearrange("p (t d) -> p t d", d=D)
        agg_hm = big[:, 0:2 * SB * COLS].rearrange("p (b s c) -> p b s c", b=2, s=SB)
        agg_lo = big[:, 2 * SB * COLS:3 * SB * COLS].rearrange("p (b s c) -> p b s c", b=2, s=SB)
        t_sb = big[:, :].rearrange("p (t c) -> p t c", t=GT)
        big2 = sb("big2", [P, NT * P])
        parts = big2[:, 0:NT * ROW // 2].bitcast(BF16).rearrange("p (t c) -> p t c", t=NT)
        iota_nodes = big2
        res = sb("res", [P, NT, D])
        ghT = msg[0:D, 0, :, :].rearrange("d k c -> d (k c)")[:, 0:2 * GT * P].bitcast(F32).rearrange("d (t p) -> d t p", t=GT)
        gh = msg[:, 1, :, :].rearrange("p k c -> p (k c)")[:, 0:2 * GT * D].bitcast(F32).rearrange("p (t d) -> p t d", t=GT)
        gmsg = msg[:, 1, :, :].rearrange("p k c -> p (k c)")[:, 0:2 * GST * D].bitcast(F32).rearrange("p (t d) -> p t d", t=GST)
        gonehot = sb("gonehot", [P, GST, P])

        ps = [ctx.enter_context(nc.psum_tensor(f"ps{i}", [P, BANK], F32)) for i in range(8)]
        ps_hm, ps_lo, ps_fl, ps_iota = ps[0:2], ps[2:4], ps[4:6], ps[7]

        s_pad, s_id, s_iota, s_acc = sem("s_pad"), sem("s_id"), sem("s_iota"), sem("s_acc")
        CH = ((0, 25), (25, NT))
        s_x = [sem(f"s_x{c}") for c in range(2)]
        s_w = sem("s_w")
        s_dst, s_src, s_typ = sem("s_dst"), sem("s_src"), sem("s_typ")
        s_minmax, s_minmaxT, s_base, s_spread, s_spreadT, s_flag, s_key, s_keyT = (
            sem(f"s_{n}") for n in ("minmax", "minmaxT", "base", "spread", "spreadT", "flag", "key", "keyT"))
        s_link = sem("s_link")
        s_idx, s_idxT, s_idxE, s_keyE = sem("s_idx"), sem("s_idxT"), sem("s_idxE"), sem("s_keyE")
        s_base_row = sem("s_base_row")
        s_ln = sem("s_ln")
        s_cent, s_sq, s_var, s_std, s_h, s_hi, s_r1, s_mid, s_parts = (
            sem(f"s_{n}") for n in ("cent", "sq", "var", "std", "h", "hi", "r1", "mid", "parts"))
        s_table = [sem(f"s_table{c}") for c in range(2)]
        s_g = [[sem(f"s_g{b}_{k}") for k in range(BT)] for b in range(2)]
        s_ks = sem("s_ks")
        s_ix, s_oh, s_sup, s_eh, s_el, s_fl, s_add = (sem(f"s_{n}") for n in ("ix", "oh", "sup", "eh", "el", "fl", "add"))
        s_prep, s_prepT, s_prepE = sem("s_gprep"), sem("s_gprepT"), sem("s_gprepE")
        s_gh, s_hp, s_hT, s_mmT = sem("s_gh"), sem("s_hp"), sem("s_hT"), sem("s_mmT")
        s_ev = [sem("s_ev_act"), sem("s_ev_dve")]
        s_tw = [sem(f"s_tw{k}") for k in range(GT)]
        s_gg = [sem(f"s_gg{k}") for k in range(GST)]
        s_gix, s_goh, s_gmm, s_gadd = (sem(f"s_{n}") for n in ("gix", "goh", "gmm", "gadd"))
        s_oT, s_res, s_out = sem("s_oT"), sem("s_res"), sem("s_out")

        halves = ((0, 4), (4, GT))
        key_banks = tuple((b, min(b + 4, EB)) for b in range(0, EB, 4))
        last_rows = lambda tile, tiles, whole: EREM if tiles < whole and tile == tiles - 1 else P

        def load_edges(eng, arr, nat, s):
            eng.dma_start(nat[:, 0:EBFULL, :],
                          arr[0:EBFULL * P * P].rearrange("(b q p) -> q b p", q=P, p=P)).then_inc(s, 16)
            eng.dma_start(nat[0:RESTQ, EBFULL, :],
                          arr[EBFULL * P * P:ETFULL * P].rearrange("(q p) -> q p", p=P)).then_inc(s, 16)
            eng.dma_start(nat[RESTQ:RESTQ + 1, EBFULL, 0:EREM],
                          arr[ETFULL * P:E].rearrange("(q p) -> q p", q=1)).then_inc(s, 16)

        def fast_or_general(eng, fast, general):
            wait(eng, s_flag, 1)
            greatest = eng.value_load(span_all[0:1, 0:1], min_val=0, max_val=N)
            with eng.If(greatest < WIN):
                fast(eng)
            with eng.Else():
                general(eng)

        block = ctx.enter_context(nc.Block())

        @block.sync
        def _(sp):
            wait(sp, s_pad, 4)
            load_edges(sp, dst, nat_dst, s_dst)
            sp.dma_start(nat_dst[RESTQ:RESTQ + 1, EBFULL, EREM:P],
                         dst[ETFULL * P:E].rearrange("(q p) -> q p", q=1)).then_inc(s_dst, 16)
            for part in range(2):
                sp.dma_start(nat_dst[RESTQ + 1:RESTQ + 2, EBFULL, part * EREM:(part + 1) * EREM],
                             dst[ETFULL * P:E].rearrange("(q p) -> q p", q=1)).then_inc(s_dst, 16)
            load_edges(sp, src, nat_src, s_src)
            load_edges(sp, etype, nat_typ, s_typ)
            wait(sp, s_base, 1)
            sp.dma_start(base_row[:, :].rearrange("o (b s) -> o b s", b=EB), super_base[:, :]).then_inc(s_base_row, 16)
            for c, (a, b) in enumerate(CH):
                wait(sp, s_parts, c + 1)
                sp.dma_start(parts_dram[a * P:b * P, :].rearrange("(t p) c -> p t c", p=P),
                             parts[:, a:b, :]).then_inc(s_table[c], 16)

            def general(sp):
                with sp.Fori(0, NG) as g:
                    for k in range(GT):
                        for s in s_ev:
                            wait(sp, s, g * GT + k + 1)
                        rows = table.rearrange("(t p r) d -> t p (r d)", p=P, r=R)[bass.ds(g * GT + k, 1)]
                        sp.dma_start(rows.rearrange("o p c -> (o p) c"), t_sb[:, k, :]).then_inc(s_tw[k], 16)

            fast_or_general(sp, lambda sp: None, general)

            full = NREM // 16 * 16
            for g in range(NG):
                t0, t1 = g * GT, min((g + 1) * GT, NT - 1)
                wait(sp, s_res, g + 1)
                sp.dma_start(out[t0 * P:t1 * P, :].rearrange("(t p) d -> p t d", p=P), res[:, t0:t1, :]).then_inc(s_out, 16)
            t0 = (NT - 1) * P
            sp.dma_start(out[t0:t0 + full, :], res[0:full, NT - 1, :]).then_inc(s_out, 16)
            sp.dma_start(out[t0 + full:N, :], res[full:NREM, NT - 1, :]).then_inc(s_out, 16)
            wait(sp, s_out, 16 * (NG + 2))

        @block.gpsimd
        def _(pool):
            pool.memset(x_sb[:, NT - 1, :], 0.0).then_inc(s_pad, 1)
            for nat in (nat_dst, nat_src, nat_typ):
                pool.memset(nat[:, EBFULL, :], 0).then_inc(s_pad, 1)
            pool.memset(ident[:, :], 0.0).then_inc(s_id, 1)
            wait(pool, s_id, 1)
            pool.affine_select(out=ident[:, :], in_=ident[:, :], compare_op=ALU.not_equal, fill=1.0, base=0,
                               pattern=[[-1, P]], channel_multiplier=1).then_inc(s_id, 1)
            pool.iota(res[:, 0:COLS // D, :].rearrange("p t d -> p (t d)"), [[1, COLS]], base=0, channel_multiplier=0,
                      allow_small_or_imprecise_dtypes=True).then_inc(s_iota, 1)
            wait(pool, s_idxE, len(key_banks))
            for s in s_table:
                wait(pool, s, 16)

            def fast(pool):
                def gather(n, b, tiles=BT):
                    hold(pool, s_ix, n + 1)
                    for k in range(tiles):
                        rows = last_rows(k, tiles, BT)
                        pool.indirect_dma_start(
                            out=msg[0:rows, b, k, :], out_offset=None, in_=parts_dram,
                            in_offset=bass.IndirectOffsetOnAxis(ap=idx_slot[0:rows, b, k:k + 1], axis=0),
                        ).then_inc(s_g[b][k], 16)

                gather(0, 0)
                with pool.Fori(0, NB // 2) as i:
                    gather(2 * i + 1, 1)
                    gather(2 * i + 2, 0)
                gather(NB, 1, LT)

            def general(pool):
                pool.iota(iota_nodes[:, :], [[1, NT * P]], base=0, channel_multiplier=0,
                          allow_small_or_imprecise_dtypes=True).then_inc(s_iota, 1)
                for k in range(GT):
                    wait(pool, s_tw[k], 16 * NG)

                def gather(s, tiles=GST):
                    hold(pool, s_gix, s + 1)
                    for k in range(tiles):
                        rows = last_rows(k, tiles, GST)
                        pool.indirect_dma_start(
                            out=gmsg[0:rows, k, :], out_offset=None, in_=table,
                            in_offset=bass.IndirectOffsetOnAxis(ap=idx_slot[0:rows, 0, k:k + 1], axis=0),
                        ).then_inc(s_gg[k], 16)

                with pool.Fori(0, GS) as s:
                    gather(s)
                gather(GS, GTAIL)

            fast_or_general(pool, fast, general)

        @block.scalar
        def _(act):
            full = NREM // 16 * 16
            t0 = (NT - 1) * P
            for c, (a, b) in enumerate(CH):
                b = min(b, NT - 1)
                act.dma_start(x_sb[:, a:b, :], x[a * P:b * P, :].rearrange("(t p) d -> p t d", p=P)).then_inc(s_x[c], 16)
            wait(act, s_pad, 4)
            act.dma_start(x_sb[0:full, NT - 1, :], x[t0:t0 + full, :]).then_inc(s_x[1], 16)
            act.dma_start(x_sb[full:NREM, NT - 1, :], x[t0 + full:N, :]).then_inc(s_x[1], 16)

            wait(act, s_src, 48)
            act.copy(nat_a[:, :, :], nat_src[:, :, :]).then_inc(s_idx, 1)

            for c, (a, b) in enumerate(CH):
                wait(act, s_cent, c + 1)
                act.activation(squares[:, a:b, :], centred[:, a:b, :], ACT.Square).then_inc(s_sq, 1)
            for n, (a, b) in enumerate(key_banks):
                wait(act, s_idxT, n + 1)
                act.copy(row_idx[:, a * P:b * P], ps[n][:, 0:(b - a) * P]).then_inc(s_idxE, 1)
            for c, (a, b) in enumerate(CH):
                wait(act, s_var, c + 1)
                act.activation(stat_std[:, a:b], stat_var[:, a:b], ACT.Sqrt).then_inc(s_std, 1)
            for c, (a, b) in enumerate(CH):
                wait(act, s_h, c + 1)
                act.copy(parts[:, a:b, 0:D], h_sb[:, a:b, :]).then_inc(s_hi, 1)
            for c, (a, b) in enumerate(CH):
                wait(act, s_r1, c + 1)
                act.copy(parts[:, a:b, D:2 * D], centred[:, a:b, :]).then_inc(s_mid, 1)
            for half in range(2):
                act.dma_start(w_hm[half * D:(half + 1) * D, :, :], weight.rearrange("r i o -> i r o")).then_inc(s_w, 16)
                act.dma_start(w_lo[half * D:(half + 1) * D, :, :],
                              weight[half * R // 2:(half + 1) * R // 2].rearrange("r i o -> i r o")).then_inc(s_w, 16)
            for n, (a, b) in enumerate(key_banks):
                wait(act, s_keyT, n + 1)
                act.copy(key[:, a * P:b * P], ps[n][:, 0:(b - a) * P]).then_inc(s_keyE, 1)
            wait(act, s_iota, 1)
            act.copy(ps_iota[:, 0:COLS], res[:, 0:COLS // D, :].rearrange("p t d -> p (t d)")).then_inc(s_keyE, 1)

            def fast(act):
                def fill_slots(n, b):
                    act.copy(idx_slot[:, b, :], row_idx[:, bass.ds(n * BT, BT)]).then_inc(s_ix, 1)
                    act.copy(key_slot[:, b, :], key[:, bass.ds(n * BT, BT)]).then_inc(s_ks, 1)

                def evacuate(n, b, supers=SB):
                    wait(act, s_fl, n - 1)
                    for j in range(supers):
                        for per_bank, banks, agg, s, cols in ((HMB, ps_hm, agg_hm, s_eh, COLS), (LOB, ps_lo, agg_lo, s_el, COLS // 2)):
                            if (j + 1) % per_bank and j + 1 < supers:
                                continue
                            wait(act, s_sup, n * SB + j + 1)
                            if supers == SB and (j, per_bank) == (HMB - 1, HMB):
                                fill_slots(n + 1, 1 - b)
                            q, a = j // per_bank, j // per_bank * per_bank
                            act.copy(agg[:, b, a:j + 1, :],
                                     banks[q % 2][:, 0:(j + 1 - a) * cols].rearrange("p (s c) -> p s c", c=cols)).then_inc(s, 1)

                wait(act, s_idxE, len(key_banks))
                wait(act, s_keyE, len(key_banks) + 1)
                fill_slots(0, 0)
                evacuate(0, 0)
                evacuate(1, 1)
                with act.Fori(1, NB // 2) as i:
                    for b in range(2):
                        evacuate(2 * i + b, b)
                evacuate(NB - 1, 0)
                evacuate(NB, 1, LS)

            def general(act):
                for n, (a, b) in enumerate(key_banks):
                    wait(act, s_prepT, n + 1)
                    act.copy(row_idx[:, a * P:b * P], ps[n][:, 0:(b - a) * P])
                    act.copy(key[:, a * P:b * P], ps[4 + n % 3][:, 0:(b - a) * P]).then_inc(s_prepE, 1)

                def group(g):
                    wait(act, s_hp, 2 * g)
                    act.copy(gh[:, :, :], h_sb[:, bass.ts(g, GT), :]).then_inc(s_gh, 1)
                    for part, (a, b) in enumerate(halves):
                        wait(act, s_hp, 2 * g + part + 1)
                        if part == 0:
                            wait(act, s_mmT, 2 * GT * g)
                        act.copy(ghT[:, a:b, :].rearrange("d t p -> d (t p)"), ps[part][0:D, 0:(b - a) * P]).then_inc(s_hT, 1)
                    for k in range(GT):
                        wait(act, s_mmT, 2 * (g * GT + k) + 1)
                        wait(act, s_tw[k], 16 * g)
                        act.copy(t_sb[:, k, 0:HALF], ps[2 + k % 2][:, 0:HALF]).then_inc(s_ev[0], 1)

                group(0)
                with act.Fori(1, NG) as g:
                    group(g)

            fast_or_general(act, fast, general)

        @block.vector
        def _(dve):
            linked = [0]

            def link(ins, s=s_link):
                linked[0] += 1
                ins.then_inc(s, 1)
                wait(dve, s, linked[0])

            wait(dve, s_dst, 16 * 6)
            dve.tensor_reduce(tile_min[:, :], nat_dst[:, :, :], AX, ALU.min)
            dve.tensor_reduce(tile_max[:, :], nat_dst[:, :, :], AX, ALU.max).then_inc(s_minmax, 1)

            for c, (a, b) in enumerate(CH):
                wait(dve, s_x[c], 16 + 32 * c)
                dve.tensor_reduce(stat_sum[:, a:b], x_sb[:, a:b, :], AX, ALU.add).then_inc(s_ln, 1)
                wait(dve, s_ln, 2 * c + 1)
                dve.tensor_scalar(stat_mean[:, a:b], stat_sum[:, a:b], 1.0 / D, None, ALU.mult).then_inc(s_ln, 1)
                wait(dve, s_ln, 2 * c + 2)
                dve.tensor_tensor(centred[:, a:b, :], x_sb[:, a:b, :], spread(stat_mean[:, a:b], D),
                                  ALU.subtract).then_inc(s_cent, 1)

            wait(dve, s_minmaxT, 1)
            pairs = lambda t: t.rearrange("b (s t) -> b s t", t=ST)
            dve.tensor_reduce(super_min[:, :], pairs(ps[4][0:EB, 0:P]), AX, ALU.min)
            link(dve.tensor_reduce(super_max[:, :], pairs(ps[4][0:EB, P:2 * P]), AX, ALU.max))
            dve.tensor_copy(super_base[:, :], super_min[:, :]).then_inc(s_base, 1)
            dve.tensor_copy(pairs(base_spread[:, :]), spread(super_min[:, :], ST))
            link(dve.tensor_tensor(super_span[:, :], super_max[:, :], super_min[:, :], ALU.subtract))
            dve.tensor_reduce(span[:, :], super_span[:, :], AX, ALU.max).then_inc(s_spread, 1)

            for c, (a, b) in enumerate(CH):
                wait(dve, s_sq, c + 1)
                dve.tensor_reduce(stat_sq[:, a:b], squares[:, a:b, :], AX, ALU.add).then_inc(s_ln, 1)
                wait(dve, s_ln, 4 + c + 1)
                dve.tensor_scalar(stat_var[:, a:b], stat_sq[:, a:b], 1.0 / D, EPS, ALU.mult, ALU.add).then_inc(s_var, 1)

            wait(dve, s_spreadT, 1)
            link(dve.tensor_copy(base_nat[:, :], ps[5][:, 0:EB]))
            dve.tensor_reduce(span_all[:, :], ps[5][0:1, P:P + EB], AX, ALU.max).then_inc(s_flag, 1)

            for c, (a, b) in enumerate(CH):
                wait(dve, s_std, c + 1)
                dve.reciprocal(stat_rstd[:, a:b], stat_std[:, a:b]).then_inc(s_ln, 1)
                wait(dve, s_ln, 6 + c + 1)
                dve.scalar_tensor_tensor(h_sb[:, a:b, :], centred[:, a:b, :], 0.0, spread(stat_rstd[:, a:b], D),
                                         ALU.max, ALU.mult).then_inc(s_h, 1)
            for c, (a, b) in enumerate(CH):
                wait(dve, s_hi, c + 1)
                dve.tensor_tensor(centred[:, a:b, :], h_sb[:, a:b, :], parts[:, a:b, 0:D], ALU.subtract).then_inc(s_r1, 1)
            for c, (a, b) in enumerate(CH):
                wait(dve, s_mid, c + 1)
                dve.tensor_tensor(parts[:, a:b, 2 * D:], centred[:, a:b, :], parts[:, a:b, D:2 * D],
                                  ALU.subtract).then_inc(s_parts, 1)

            wait(dve, s_typ, 48)
            link(dve.tensor_tensor(nat_b[:, :, :], nat_dst[:, :, :], spread(base_nat[:, :], P), ALU.subtract))
            dve.scalar_tensor_tensor(nat_b[:, :, :].rearrange("q b p -> q (b p)"), nat_typ[:, :, :].rearrange("q b p -> q (b p)"),
                                     float(WIN), nat_b[:, :, :].rearrange("q b p -> q (b p)"), ALU.mult, ALU.add).then_inc(s_key, 1)
            dve.memset(accT[:, :], 0.0).then_inc(s_acc, 1)
            wait(dve, s_idxE, len(key_banks))

            def fast(dve):
                wait(dve, s_base_row, 16)
                wait(dve, s_keyE, len(key_banks) + 1)

                def one_hots(n, b, j, tiles=ST):
                    wait(dve, s_sup, n * SB + j - RING + 1)
                    for t in range(tiles):
                        last = dve.tensor_scalar(onehot[:, j % RING * ST + t, :], ps_iota[:, 0:COLS],
                                                 key_slot[:, b, j * ST + t:j * ST + t + 1], None, ALU.is_equal)
                    last.then_inc(s_oh, 1)

                def add_windows(n, b, windows):
                    wait(dve, s_fl, n + 1)
                    _, bases = nc.values_load_multi_w_load_instructions(
                        base_row[0:1, bass.ds(n * SB + windows[0], len(windows))],
                        engines=[dve.engine], min_val=0, max_val=N)
                    for j, base in zip(windows, bases):
                        wait(dve, s_add, n * SB + j)
                        here = accT[:, bass.ds(base, WIN)]
                        dve.tensor_tensor(here, here, ps_fl[b][0:D, j * WIN:(j + 1) * WIN], ALU.add).then_inc(s_add, 1)

                def batch(n, b, tiles=BT, after=None):
                    supers = -(-tiles // ST)
                    adds = {6: range(4), 7: range(4, SB)} if supers == SB else {supers - 1: range(SB)}
                    wait(dve, s_ks, n + 1)
                    for j in range(supers):
                        one_hots(n, b, j, min(ST, tiles - j * ST))
                        if j in adds and (not isinstance(n, int) or n > 0):
                            add_windows(n - 1, 1 - b, adds[j])

                batch(0, 0)
                with dve.Fori(0, NB // 2) as i:
                    batch(2 * i + 1, 1)
                    batch(2 * i + 2, 0)
                batch(NB, 1, LT)
                add_windows(NB, 1, range(LS))

            def general(dve):
                row_of = lambda t: t[:, :, :].rearrange("q b p -> q (b p)")
                wait(dve, s_keyT, len(key_banks))
                dve.scalar_tensor_tensor(row_of(nat_a), row_of(nat_src), float(R), row_of(nat_typ), ALU.mult, ALU.add)
                dve.tensor_copy(nat_b[:, :, :], nat_dst[:, :, :]).then_inc(s_prep, 1)

                def group(g):
                    for k in range(GT):
                        wait(dve, s_mmT, 2 * (g * GT + k) + 2)
                        wait(dve, s_tw[k], 16 * g)
                        dve.tensor_copy(t_sb[:, k, HALF:], ps[4 + k % 2][:, 0:HALF]).then_inc(s_ev[1], 1)

                group(0)
                with dve.Fori(1, NG) as g:
                    group(g)
                wait(dve, s_iota, 2)
                wait(dve, s_prepE, len(key_banks))

                with dve.Fori(0, GS + 1) as s:
                    dve.tensor_copy(idx_slot[:, 0, 0:GST], row_idx[:, bass.ts(s, GST)]).then_inc(s_gix, 1)
                    with dve.Fori(0, NT) as w:
                        u = s * NT + w
                        nodes = iota_nodes[:, bass.ts(w, P)].rearrange("p (o w) -> p o w", o=1).to_broadcast([P, GST, P])
                        dve.tensor_tensor(gonehot[:, :, :], nodes, spread(key[:, bass.ts(s, GST)], P),
                                          ALU.is_equal).then_inc(s_goh, 1)
                        wait(dve, s_gmm, u + 1)
                        here = accT[:, bass.ts(w, P)]
                        dve.tensor_tensor(here, here, ps[0][0:D, 0:P], ALU.add).then_inc(s_gadd, 1)
                        wait(dve, s_gadd, u + 1)

            fast_or_general(dve, fast, general)
            wait(dve, s_acc, 1)
            dve.memset(stat_sum[:, 0:1], 0.0).then_inc(s_acc, 1)

            for g in range(NG):
                wait(dve, s_oT, g + 1)
                tiles = slice(g * GT, (g + 1) * GT)
                dve.tensor_tensor(res[:, tiles, :], ps[g % 4][:, 0:GT * D].rearrange("p (t d) -> p t d", d=D),
                                  x_sb[:, tiles, :], ALU.add).then_inc(s_res, 1)

        @block.tensor
        def _(pe):
            def turn(nat, banks, ready, done):
                for n, (a, b) in enumerate(key_banks):
                    for k in range(a, b):
                        last = pe.transpose(banks(n)[:, (k - a) * P:(k - a + 1) * P], nat[:, k, :], ident[:, :])
                    last.then_inc(done, 1)

            wait(pe, s_id, 2)
            wait(pe, s_minmax, 1)
            pe.transpose(ps[4][0:EB, 0:P], tile_min[:, :], ident[:, :])
            pe.transpose(ps[4][0:EB, P:2 * P], tile_max[:, :], ident[:, :]).then_inc(s_minmaxT, 1)
            wait(pe, s_idx, 1)
            turn(nat_a, lambda n: ps[n], s_idx, s_idxT)
            wait(pe, s_spread, 1)
            pe.transpose(ps[5][:, 0:EB], base_spread[:, :], ident[0:EB, 0:EB])
            pe.transpose(ps[5][0:1, P:P + EB], span[:, :], ident[0:EB, 0:EB]).then_inc(s_spreadT, 1)
            wait(pe, s_key, 1)
            wait(pe, s_idxE, len(key_banks))
            turn(nat_b, lambda n: ps[n], s_key, s_keyT)

            def fast(pe):
                wait(pe, s_w, 64)
                wait(pe, s_keyE, len(key_banks) + 1)

                def sum_super(n, b, j, tiles=ST):
                    q, u = n * (SB // HMB) + j // HMB, n * (SB // LOB) + j // LOB
                    hm = ps_hm[j // HMB % 2][:, j % HMB * COLS:(j % HMB + 1) * COLS]
                    lo = ps_lo[j // LOB % 2][:, j % LOB * COLS // 2:(j % LOB + 1) * COLS // 2]
                    if j % HMB == 0:
                        wait(pe, s_eh, q - 1)
                    if j % LOB == 0:
                        wait(pe, s_el, u - 1)
                    wait(pe, s_oh, n * SB + j + 1)
                    for t in range(tiles):
                        k = j * ST + t
                        rows = EREM if tiles < ST else P
                        wait(pe, s_g[b][k], 16 * (n // 2 + 1) if isinstance(n, int) else 8 * n + (16 - 8 * b))
                        start, stop = t == 0, t == tiles - 1
                        hot = onehot[0:rows, j % RING * ST + t, :]
                        pe.matmul(hm, msg[0:rows, b, k, 0:P], hot, start=start, stop=stop)
                        for half in range(2):
                            last = pe.matmul(lo[half * D:(half + 1) * D, :], msg[0:rows, b, k, P:ROW],
                                             hot[:, half * COLS // 2:(half + 1) * COLS // 2], start=start, stop=stop)
                    last.then_inc(s_sup, 1)

                def weigh(n, b, supers=SB):
                    wait(pe, s_eh, n * (SB // HMB) + -(-supers // HMB))
                    wait(pe, s_el, n * (SB // LOB) + -(-supers // LOB))
                    wait(pe, s_add, (n - 1) * SB)
                    fl = ps_fl[b][0:D, 0:supers * WIN]
                    for r in range(R):
                        pe.matmul(fl, w_hm[:, r, :], agg_hm[:, b, 0:supers, r * WIN:(r + 1) * WIN], start=r == 0, stop=False)
                    for r in range(R // 2):
                        last = pe.matmul(fl, w_lo[:, r, :], agg_lo[:, b, 0:supers, r * WIN:(r + 1) * WIN],
                                         start=False, stop=r == R // 2 - 1)
                    last.then_inc(s_fl, 1)

                def batch(n, b, tiles=BT):
                    for j in range(-(-tiles // ST)):
                        sum_super(n, b, j, min(ST, tiles - j * ST))
                        if j == 1 and (not isinstance(n, int) or n > 0):
                            weigh(n - 1, 1 - b)

                batch(0, 0)
                batch(1, 1)
                batch(2, 0)
                with pe.Fori(1, NB // 2) as i:
                    batch(2 * i + 1, 1)
                    batch(2 * i + 2, 0)
                batch(NB, 1, LT)
                weigh(NB, 1, LS)

            def general(pe):
                wait(pe, s_keyE, len(key_banks) + 1)
                wait(pe, s_prep, 1)
                for n, (a, b) in enumerate(key_banks):
                    if n == 3:
                        wait(pe, s_prepE, 1)
                    for nat, bank in ((nat_a, ps[n]), (nat_b, ps[4 + n % 3])):
                        for k in range(a, b):
                            last = pe.transpose(bank[:, (k - a) * P:(k - a + 1) * P], nat[:, k, :], ident[:, :])
                    last.then_inc(s_prepT, 1)
                wait(pe, s_prepE, len(key_banks))
                wait(pe, s_w, 64)

                def group(g):
                    hold(pe, s_gh, g + 1)
                    hold(pe, s_hT, 2 * g)
                    for part, (a, b) in enumerate(halves):
                        for k in range(a, b):
                            last = pe.transpose(ps[part][0:D, (k - a) * P:(k - a + 1) * P], gh[:, k, :], ident[:, :])
                        last.then_inc(s_hp, 1)
                    for k in range(GT):
                        if k in (0, 4):
                            hold(pe, s_hT, 2 * g + (1 if k == 0 else 2))
                        n = g * GT + k
                        prev = n - 1 if k > 1 else n - 2 if k == 1 else n
                        for half in range(2):
                            wait(pe, s_ev[half], prev)
                            pe.matmul(ps[2 + 2 * half + k % 2][:, 0:HALF], ghT[:, k, :],
                                      w_hm[0:D, half * R // 2:(half + 1) * R // 2, :].rearrange("i r o -> i (r o)"),
                                      start=True, stop=True).then_inc(s_mmT, 1)

                group(0)
                with pe.Fori(1, NG) as g:
                    group(g)

                def supertile(s, tiles=GST):
                    for k in range(tiles):
                        hold(pe, s_gg[k], 16 * (s + 1))
                    with pe.Fori(0, NT) as w:
                        wait(pe, s_goh, s * NT + w + 1)
                        for k in range(tiles):
                            rows = last_rows(k, tiles, GST)
                            last = pe.matmul(ps[0][0:D, 0:P], gmsg[0:rows, k, :], gonehot[0:rows, k, :],
                                             start=(k == 0), stop=(k == tiles - 1))
                        last.then_inc(s_gmm, 1)

                with pe.Fori(0, GS) as s:
                    supertile(s)
                supertile(GS, GTAIL)

            fast_or_general(pe, fast, general)

            wait(pe, s_acc, 2)
            for g in range(NG):
                wait(pe, s_res, g - 3)
                for k in range(GT):
                    t = g * GT + k
                    last = pe.transpose(ps[g % 4][:, k * D:(k + 1) * D], accT[:, t * P:(t + 1) * P], ident[0:D, 0:D])
                last.then_inc(s_oT, 1)


def kernel(x, src, dst, edge_type_16, L0_gnn_weight):
    from concourse import bacc
    from concourse.bass_utils import run_bass_kernel_spmd

    given = {"x": x, "src": src, "dst": dst, "edge_type": edge_type_16, "weight": L0_gnn_weight}
    arrays = {name: np.ascontiguousarray(a) for name, a in given.items()}
    nc = bacc.Bacc("TRN2", target_bir_lowering=False, num_devices=1)
    aps = [nc.dram_tensor(name, a.shape, mybir.dt.from_np(a.dtype), kind="ExternalInput").ap()
           for name, a in arrays.items()]
    out = nc.dram_tensor("out", arrays["x"].shape, F32, kind="ExternalOutput").ap()
    gnn_program(nc, *aps, out)
    run = run_bass_kernel_spmd(nc, [arrays], core_ids=[0])
    return run.results[0]["out"]
```

```python
from contextlib import ExitStack

import numpy as np
import concourse.bass as bass
import concourse.mybir as mybir

F32 = mybir.dt.float32
BF16 = mybir.dt.bfloat16
I32 = mybir.dt.int32
ALU = mybir.AluOpType
ACT = mybir.ActivationFunctionType
AX = mybir.AxisListType.X
P = 128
EPS = 1e-5
BANK = 512


def wait(eng, sem, value):
    if not isinstance(value, int) or value > 0:
        eng.wait_ge(sem, value)


def hold(eng, sem, value):
    wait(eng, sem, value)
    if not isinstance(value, int):
        eng.nop(nofuse=True)


def spread(t, n):
    return t.rearrange("p (m o) -> p m o", o=1).to_broadcast([t.shape[0], t.shape[1], n])


def gnn_program(nc, x, src, dst, etype, weight, out):
    N, D = x.shape
    E = src.shape[0]
    R = weight.shape[0]
    NT = -(-N // P)
    FULLP = N // NT
    NREM = N - FULLP * NT
    GT = 7
    NG = NT // GT
    NPART = 3
    ROW = NPART * D
    assert NG * GT == NT and 2 * D == P

    ET = -(-E // P)
    ETFULL = E // P
    EREM = E - ETFULL * P
    EB = -(-ET // P)
    EBFULL = E // (P * P)
    RESTQ = ETFULL - EBFULL * P
    ST = 2
    WIN = 16
    COLS = R * WIN
    SB = 8
    BT = SB * ST
    NB = ET // BT
    LT = ET - NB * BT
    LS = -(-LT // ST)
    NSB = P // ST
    RING = 4
    HMB, LOB = BANK // COLS, 2 * BANK // COLS
    OWN = BT - 1
    PIECES = ((0, 7), (7, 14), (14, 21), (21, 28), (28, 35), (35, 42), (42, NT))
    MADE_AFTER = {3: (0,), 4: (1,), 5: (2, 3), 6: (4,), 7: (5, 6)}
    USED_AFTER = {4: (0, 1), 5: (2, 3), 6: (4, 5), 7: (6,)}
    assert LT <= OWN
    assert EREM and LT and NB % 2 == 1 and SB % RING == 0 and RESTQ % ST == 0

    GST = 8
    GS = ET // GST
    GTAIL = ET - GS * GST
    HALF = R * D // 2
    assert HALF == BANK and GTAIL

    parts_dram = nc.dram_tensor("parts_dram", [NT * P, ROW], BF16).ap()
    table = nc.dram_tensor("table", [NT * P * R, D], F32).ap()

    ctx = ExitStack()
    sb = lambda name, shape, dt=F32: ctx.enter_context(nc.sbuf_tensor(name, shape, dt))
    sem = lambda name: ctx.enter_context(nc.semaphore(name))
    with ctx:
        x_sb = sb("x_sb", [P, NT, D])
        h_sb = sb("h_sb", [P, NT, D])
        w_hm = sb("w_hm", [P, R, D])
        w_lo = sb("w_lo", [P, R // 2, D])
        ident = sb("ident", [P, P])
        nat_src = sb("nat_src", [P, EB, P], I32)
        nat_typ = sb("nat_typ", [P, EB, P], I32)
        nat_dst = sb("nat_dst", [P, EB, P], I32)
        nat_a = sb("nat_a", [P, EB, P])
        nat_b = sb("nat_b", [P, EB, P])
        row_idx = sb("row_idx", [P, EB * P], I32)
        key = sb("key", [P, EB * P])
        tile_min = sb("tile_min", [P, EB])
        tile_max = sb("tile_max", [P, EB])
        super_min = sb("super_min", [EB, NSB])
        super_max = sb("super_max", [EB, NSB])
        super_base = sb("super_base", [EB, NSB], I32)
        super_span = sb("super_span", [EB, NSB])
        base_spread = sb("base_spread", [EB, P])
        base_nat = sb("base_nat", [P, EB])
        base_row = sb("base_row", [1, EB * NSB], I32)
        span = sb("span", [EB, 1])
        span_all = sb("span_all", [1, 1], I32)
        stat_sum, stat_mean, stat_sq, stat_var, stat_std, stat_rstd = (
            sb(f"stat{i}", [P, NT]) for i in range(6))
        msg = sb("msg", [P, 2, BT, ROW], BF16)
        idx_slot = sb("idx_slot", [P, 2, BT], I32)
        key_slot = sb("key_slot", [P, 2, BT])
        onehot = sb("onehot", [P, RING * ST, COLS], BF16)
        src_own = sb("src_own", [P, 2, P], I32)
        node_hot = sb("node_hot", [P, NT, P], BF16)
        node_ids = sb("node_ids", [P, NT])
        accT = sb("accT", [D, NT * P + WIN])
        big = sb("big", [P, GT * R * D])
        centred = big[:, 0:NT * D].rearrange("p (t d) -> p t d", d=D)
        squares = big[:, NT * D:2 * NT * D].rearrange("p (t d) -> p t d", d=D)
        agg_hm = big[:, 0:2 * SB * COLS].rearrange("p (b s c) -> p b s c", b=2, s=SB)
        agg_lo = big[:, 2 * SB * COLS:3 * SB * COLS].rearrange("p (b s c) -> p b s c", b=2, s=SB)
        t_sb = big[:, :].rearrange("p (t c) -> p t c", t=GT)
        big2 = sb("big2", [P, NT * P])
        parts = big2[:, 0:NT * ROW // 2].bitcast(BF16).rearrange("p (t c) -> p t c", t=NT)
        iota_nodes = big2
        res = sb("res", [P, NT, D])
        ghT = msg[0:D, 0, :, :].rearrange("d k c -> d (k c)")[:, 0:2 * GT * P].bitcast(F32).rearrange("d (t p) -> d t p", t=GT)
        gh = msg[:, 1, :, :].rearrange("p k c -> p (k c)")[:, 0:2 * GT * D].bitcast(F32).rearrange("p (t d) -> p t d", t=GT)
        gmsg = msg[:, 1, :, :].rearrange("p k c -> p (k c)")[:, 0:2 * GST * D].bitcast(F32).rearrange("p (t d) -> p t d", t=GST)
        gonehot = sb("gonehot", [P, GST, P])

        ps = [ctx.enter_context(nc.psum_tensor(f"ps{i}", [P, BANK], F32)) for i in range(8)]
        ps_hm, ps_lo, ps_fl, ps_own, ps_iota = ps[0:2], ps[2:4], ps[4:6], ps[6], ps[7]
        ps_nodes = ps_iota[:, COLS:COLS + NT]

        s_pad, s_id, s_iota, s_acc = sem("s_pad"), sem("s_id"), sem("s_iota"), sem("s_acc")
        CH = ((0, 14), (14, 37), (37, NT))
        s_x = [sem(f"s_x{c}") for c in range(len(CH))]
        s_w = sem("s_w")
        s_dst, s_src, s_typ = sem("s_dst"), sem("s_src"), sem("s_typ")
        s_minmax, s_minmaxT, s_base, s_spread, s_spreadT, s_flag, s_key, s_keyT = (
            sem(f"s_{n}") for n in ("minmax", "minmaxT", "base", "spread", "spreadT", "flag", "key", "keyT"))
        s_consts = sem("s_consts")
        s_link = sem("s_link")
        s_idx, s_idxT, s_idxE, s_keyE = sem("s_idx"), sem("s_idxT"), sem("s_idxE"), sem("s_keyE")
        s_base_row = sem("s_base_row")
        s_ln = sem("s_ln")
        s_cent, s_sq, s_var, s_std, s_h, s_hi, s_r1, s_mid, s_parts = (
            sem(f"s_{n}") for n in ("cent", "sq", "var", "std", "h", "hi", "r1", "mid", "parts"))
        s_table = [sem(f"s_table{c}") for c in range(len(CH))]
        s_g = [[sem(f"s_g{b}_{k}") for k in range(BT)] for b in range(2)]
        s_ks = sem("s_ks")
        s_own_src = [sem(f"s_own_src{b}") for b in range(2)]
        s_own_hot = sem("s_own_hot")
        s_own_sum = sem("s_own_sum")
        s_own = sem("s_own")
        s_ix = sem("s_ix")
        s_oh = sem("s_oh")
        s_sup = sem("s_sup")
        s_eh, s_el = sem("s_eh"), sem("s_el")
        s_fl = sem("s_fl")
        s_add = sem("s_add")
        s_prep, s_prepT, s_prepE = sem("s_gprep"), sem("s_gprepT"), sem("s_gprepE")
        s_gh, s_hp, s_hT, s_mmT = sem("s_gh"), sem("s_hp"), sem("s_hT"), sem("s_mmT")
        s_ev = [sem("s_ev_act"), sem("s_ev_dve")]
        s_tw = [sem(f"s_tw{k}") for k in range(GT)]
        s_gg = [sem(f"s_gg{k}") for k in range(GST)]
        s_gix, s_goh, s_gmm, s_gadd = (sem(f"s_{n}") for n in ("gix", "goh", "gmm", "gadd"))
        s_oT, s_res, s_out = sem("s_oT"), sem("s_res"), [sem("s_out_sp"), sem("s_out_act")]

        halves = ((0, 4), (4, GT))
        key_banks = tuple((b, min(b + 4, EB)) for b in range(0, EB, 4))
        last_rows = lambda tile, tiles, whole: EREM if tiles < whole and tile == tiles - 1 else P

        STRIPS = ((0, FULLP // 16 * 16), (FULLP // 16 * 16, FULLP))

        def nodes_of(dram, strip, a, b):
            lo, hi = STRIPS[strip]
            return dram[lo * NT:hi * NT, :].rearrange("(p t) d -> p t d", t=NT)[:, a:b, :]

        def load_x(eng, c):
            a, b = CH[c]
            for strip, (lo, hi) in enumerate(STRIPS):
                eng.dma_start(x_sb[lo:hi, a:b, :], nodes_of(x, strip, a, b)).then_inc(s_x[c], 16)
            if a < NREM:
                last = slice(FULLP * NT + a, FULLP * NT + min(b, NREM))
                eng.dma_start(x_sb[FULLP:FULLP + 1, a:min(b, NREM), :],
                              x[last, :].rearrange("(p t) d -> p t d", p=1)).then_inc(s_x[c], 16)

        x_dmas = [len(STRIPS) + (a < NREM) for a, b in CH]
        edge_dmas = 3

        def fill_idx(act, n, b):
            act.copy(idx_slot[:, b, :], row_idx[:, bass.ds(n * BT, BT)]).then_inc(s_ix, 1)

        def load_edges(eng, arr, nat, s):
            eng.dma_start(nat[:, 0:EBFULL, :],
                          arr[0:EBFULL * P * P].rearrange("(b q p) -> q b p", q=P, p=P)).then_inc(s, 16)
            eng.dma_start(nat[0:RESTQ, EBFULL, :],
                          arr[EBFULL * P * P:ETFULL * P].rearrange("(q p) -> q p", p=P)).then_inc(s, 16)
            eng.dma_start(nat[RESTQ:RESTQ + 1, EBFULL, 0:EREM],
                          arr[ETFULL * P:E].rearrange("(q p) -> q p", q=1)).then_inc(s, 16)

        def fast_or_general(eng, fast, general):
            wait(eng, s_flag, 1)
            greatest = eng.value_load(span_all[0:1, 0:1], min_val=0, max_val=N)
            with eng.If(greatest < WIN):
                fast(eng)
            with eng.Else():
                general(eng)

        def store_out(eng, strip):
            lo, hi = STRIPS[strip]
            n = 0
            for g in range(NG):
                a, b = g * GT, (g + 1) * GT
                wait(eng, s_res, g + 1)
                eng.dma_start(nodes_of(out, strip, a, b), res[lo:hi, a:b, :]).then_inc(s_out[strip], 16)
                n += 1
                if strip == 1 and a < NREM <= b:
                    eng.dma_start(out[FULLP * NT:N, :].rearrange("(p t) d -> p t d", p=1),
                                  res[FULLP:FULLP + 1, 0:NREM, :]).then_inc(s_out[strip], 16)
                    n += 1
            wait(eng, s_out[strip], 16 * n)

        block = ctx.enter_context(nc.Block())

        @block.sync
        def _(sp):
            load_x(sp, 0)
            wait(sp, s_pad, 4)
            load_edges(sp, dst, nat_dst, s_dst)
            sp.dma_start(nat_dst[RESTQ:RESTQ + 1, EBFULL, EREM:P],
                         dst[ETFULL * P:E].rearrange("(q p) -> q p", q=1)).then_inc(s_dst, 16)
            for part in range(2):
                sp.dma_start(nat_dst[RESTQ + 1:RESTQ + 2, EBFULL, part * EREM:(part + 1) * EREM],
                             dst[ETFULL * P:E].rearrange("(q p) -> q p", q=1)).then_inc(s_dst, 16)
            load_edges(sp, src, nat_src, s_src)
            for c, (a, b) in enumerate(CH):
                wait(sp, s_parts, c + 1)
                sp.dma_start(parts_dram.rearrange("(p t) c -> p t c", t=NT)[:, a:b, :],
                             parts[:, a:b, :]).then_inc(s_table[c], 16)
            wait(sp, s_base, 1)
            sp.dma_start(base_row[:, :].rearrange("o (b s) -> o b s", b=EB), super_base[:, :]).then_inc(s_base_row, 16)

            for half in range(2):
                sp.dma_start(w_hm[half * D:(half + 1) * D, :, :], weight.rearrange("r i o -> i r o")).then_inc(s_w, 16)
                sp.dma_start(w_lo[half * D:(half + 1) * D, :, :],
                              weight[half * R // 2:(half + 1) * R // 2].rearrange("r i o -> i r o")).then_inc(s_w, 16)

            def general(sp):
                with sp.Fori(0, NG) as g:
                    for k in range(GT):
                        for s in s_ev:
                            wait(sp, s, g * GT + k + 1)
                        rows = table.rearrange("(p t r) d -> t p (r d)", t=NT, r=R)[bass.ds(g * GT + k, 1)]
                        sp.dma_start(rows.rearrange("o p c -> (o p) c"), t_sb[:, k, :]).then_inc(s_tw[k], 16)

            def fast(sp):
                def load_own(n, b):
                    wait(sp, s_own_hot, len(PIECES) * (n - 2))
                    sp.dma_start(src_own[:, b, :],
                                 src[bass.ds((n * BT + OWN) * P, P)].rearrange("(o e) -> o e", o=1).to_broadcast([P, P])
                                 ).then_inc(s_own_src[b], 16)

                load_own(1, 1)
                load_own(2, 0)
                with sp.Fori(1, NB // 2) as i:
                    load_own(2 * i + 1, 1)
                    load_own(2 * i + 2, 0)

            fast_or_general(sp, fast, general)

            store_out(sp, 0)
            wait(sp, s_base_row, 16)

        @block.gpsimd
        def _(pool):
            pool.memset(x_sb[FULLP // 32 * 32:, NREM:, :], 0.0).then_inc(s_pad, 1)
            wait(pool, s_pad, 1)
            for nat in (nat_dst, nat_src, nat_typ):
                pool.memset(nat[:, EBFULL, :], 0).then_inc(s_pad, 1)
            pool.memset(ident[:, :], 0.0).then_inc(s_id, 1)
            wait(pool, s_id, 1)
            pool.affine_select(out=ident[:, :], in_=ident[:, :], compare_op=ALU.not_equal, fill=1.0, base=0,
                               pattern=[[-1, P]], channel_multiplier=1).then_inc(s_id, 1)
            pool.iota(res[:, 0:COLS // D, :].rearrange("p t d -> p (t d)"), [[1, COLS]], base=0, channel_multiplier=0,
                      allow_small_or_imprecise_dtypes=True).then_inc(s_iota, 1)
            pool.iota(node_ids[:, :], [[1, NT]], base=0, channel_multiplier=NT,
                      allow_small_or_imprecise_dtypes=True).then_inc(s_iota, 1)
            pool.memset(accT[:, :], 0.0).then_inc(s_add, 1)
            wait(pool, s_idxE, len(key_banks))
            for s in s_table:
                wait(pool, s, 16)

            def fast(pool):
                def gather(n, b, tiles=BT, first=False):
                    hold(pool, s_ix, n + 1)
                    for k in range(tiles):
                        if k == OWN and not first:
                            continue
                        rows = last_rows(k, tiles, BT)
                        pool.indirect_dma_start(
                            out=msg[0:rows, b, k, :], out_offset=None, in_=parts_dram,
                            in_offset=bass.IndirectOffsetOnAxis(ap=idx_slot[0:rows, b, k:k + 1], axis=0),
                        ).then_inc(s_g[b][k], 16)

                gather(0, 0, first=True)
                with pool.Fori(0, NB // 2) as i:
                    gather(2 * i + 1, 1)
                    gather(2 * i + 2, 0)
                gather(NB, 1, LT)

            def general(pool):
                pool.iota(iota_nodes[:, :], [[1, NT * P]], base=0, channel_multiplier=0,
                          allow_small_or_imprecise_dtypes=True).then_inc(s_iota, 1)
                for k in range(GT):
                    wait(pool, s_tw[k], 16 * NG)

                def gather(s, tiles=GST):
                    hold(pool, s_gix, s + 1)
                    for k in range(tiles):
                        rows = last_rows(k, tiles, GST)
                        pool.indirect_dma_start(
                            out=gmsg[0:rows, k, :], out_offset=None, in_=table,
                            in_offset=bass.IndirectOffsetOnAxis(ap=idx_slot[0:rows, 0, k:k + 1], axis=0),
                        ).then_inc(s_gg[k], 16)

                with pool.Fori(0, GS) as s:
                    gather(s)
                gather(GS, GTAIL)

            fast_or_general(pool, fast, general)

        @block.scalar
        def _(act):
            assert CH[1][0] <= NREM <= CH[1][1] and CH[0][1] <= NREM
            wait(act, s_pad, 1)
            for c in range(1, len(CH)):
                load_x(act, c)
            wait(act, s_pad, 4)

            load_edges(act, etype, nat_typ, s_typ)
            wait(act, s_iota, 2)
            act.copy(ps_nodes, node_ids[:, :])
            act.copy(ps_iota[:, 0:COLS], res[:, 0:COLS // D, :].rearrange("p t d -> p (t d)")).then_inc(s_consts, 1)

            for c, (a, b) in enumerate(CH):
                wait(act, s_cent, c + 1)
                act.activation(squares[:, a:b, :], centred[:, a:b, :], ACT.Square).then_inc(s_sq, 1)
            wait(act, s_src, 16 * edge_dmas)
            act.copy(nat_a[:, :, :], nat_src[:, :, :]).then_inc(s_idx, 1)
            for c, (a, b) in enumerate(CH):
                wait(act, s_var, c + 1)
                act.activation(stat_std[:, a:b], stat_var[:, a:b], ACT.Sqrt).then_inc(s_std, 1)
            for c, (a, b) in enumerate(CH):
                wait(act, s_h, c + 1)
                act.copy(parts[:, a:b, 0:D], h_sb[:, a:b, :]).then_inc(s_hi, 1)
            for c, (a, b) in enumerate(CH):
                wait(act, s_r1, c + 1)
                act.copy(parts[:, a:b, D:2 * D], centred[:, a:b, :]).then_inc(s_mid, 1)
            for n, (a, b) in enumerate(key_banks):
                wait(act, s_idxT, n + 1)
                act.copy(row_idx[:, a * P:b * P], ps[n][:, 0:(b - a) * P]).then_inc(s_idxE, 1)
                if n == 0:
                    wait(act, s_idxE, 1)
                    fill_idx(act, 0, 0)

            def take_keys(act):
                for n, (a, b) in enumerate(key_banks):
                    wait(act, s_keyT, n + 1)
                    act.copy(key[:, a * P:b * P], ps[n][:, 0:(b - a) * P]).then_inc(s_keyE, 1)

            def fast(act):
                def fill_keys(n, b):
                    act.copy(key_slot[:, b, :], key[:, bass.ds(n * BT, BT)]).then_inc(s_ks, 1)

                def evacuate(n, b, supers=SB, fetch=True):
                    wait(act, s_fl, n - 1)
                    for j in range(supers):
                        for per_bank, banks, agg, s, cols in ((HMB, ps_hm, agg_hm, s_eh, COLS), (LOB, ps_lo, agg_lo, s_el, COLS // 2)):
                            if (j + 1) % per_bank and j + 1 < supers:
                                continue
                            wait(act, s_sup, n * SB + j + 1)
                            if supers == SB and (j, per_bank) == (HMB - 1, HMB):
                                fill_idx(act, n + 1, 1 - b)
                                fill_keys(n + 1, 1 - b)
                            q, a = j // per_bank, j // per_bank * per_bank
                            act.copy(agg[:, b, a:j + 1, :],
                                     banks[q % 2][:, 0:(j + 1 - a) * cols].rearrange("p (s c) -> p s c", c=cols)).then_inc(s, 1)
                    if supers == SB and fetch:
                        wait(act, s_own_sum, n + 1)
                        act.copy(msg[:, 1 - b, OWN, :], ps_own[:, 0:ROW]).then_inc(s_own, 1)

                wait(act, s_idxE, len(key_banks))
                take_keys(act)
                wait(act, s_keyE, len(key_banks))
                fill_keys(0, 0)
                evacuate(0, 0)
                evacuate(1, 1)
                with act.Fori(1, NB // 2) as i:
                    for b in range(2):
                        evacuate(2 * i + b, b)
                evacuate(NB - 1, 0, fetch=False)
                evacuate(NB, 1, LS)

            def general(act):
                take_keys(act)
                for n, (a, b) in enumerate(key_banks):
                    wait(act, s_prepT, n + 1)
                    act.copy(row_idx[:, a * P:b * P], ps[n][:, 0:(b - a) * P])
                    act.copy(key[:, a * P:b * P], ps[4 + n % 3][:, 0:(b - a) * P]).then_inc(s_prepE, 1)

                def group(g):
                    wait(act, s_hp, 2 * g)
                    act.copy(gh[:, :, :], h_sb[:, bass.ts(g, GT), :]).then_inc(s_gh, 1)
                    for part, (a, b) in enumerate(halves):
                        wait(act, s_hp, 2 * g + part + 1)
                        if part == 0:
                            wait(act, s_mmT, 2 * GT * g)
                        act.copy(ghT[:, a:b, :].rearrange("d t p -> d (t p)"), ps[part][0:D, 0:(b - a) * P]).then_inc(s_hT, 1)
                    for k in range(GT):
                        wait(act, s_mmT, 2 * (g * GT + k) + 1)
                        wait(act, s_tw[k], 16 * g)
                        act.copy(t_sb[:, k, 0:HALF], ps[2 + k % 2][:, 0:HALF]).then_inc(s_ev[0], 1)

                group(0)
                with act.Fori(1, NG) as g:
                    group(g)

            fast_or_general(act, fast, general)
            store_out(act, 1)

        @block.vector
        def _(dve):
            linked = [0]

            def link(ins, s=s_link):
                linked[0] += 1
                ins.then_inc(s, 1)
                wait(dve, s, linked[0])

            for c, (a, b) in enumerate(CH):
                wait(dve, s_x[c], 16 * x_dmas[c])
                dve.tensor_reduce(stat_sum[:, a:b], x_sb[:, a:b, :], AX, ALU.add).then_inc(s_ln, 1)
                wait(dve, s_ln, 2 * c + 1)
                dve.tensor_scalar(stat_mean[:, a:b], stat_sum[:, a:b], 1.0 / D, None, ALU.mult).then_inc(s_ln, 1)
                wait(dve, s_ln, 2 * c + 2)
                dve.tensor_tensor(centred[:, a:b, :], x_sb[:, a:b, :], spread(stat_mean[:, a:b], D),
                                  ALU.subtract).then_inc(s_cent, 1)

            for c, (a, b) in enumerate(CH):
                wait(dve, s_sq, c + 1)
                dve.tensor_reduce(stat_sq[:, a:b], squares[:, a:b, :], AX, ALU.add).then_inc(s_ln, 1)
                wait(dve, s_ln, 2 * len(CH) + c + 1)
                dve.tensor_scalar(stat_var[:, a:b], stat_sq[:, a:b], 1.0 / D, EPS, ALU.mult, ALU.add).then_inc(s_var, 1)

            for c, (a, b) in enumerate(CH):
                wait(dve, s_std, c + 1)
                dve.reciprocal(stat_rstd[:, a:b], stat_std[:, a:b]).then_inc(s_ln, 1)
                wait(dve, s_ln, 3 * len(CH) + c + 1)
                dve.scalar_tensor_tensor(h_sb[:, a:b, :], centred[:, a:b, :], 0.0, spread(stat_rstd[:, a:b], D),
                                         ALU.max, ALU.mult).then_inc(s_h, 1)
            for c, (a, b) in enumerate(CH):
                wait(dve, s_hi, c + 1)
                dve.tensor_tensor(centred[:, a:b, :], h_sb[:, a:b, :], parts[:, a:b, 0:D], ALU.subtract).then_inc(s_r1, 1)
            for c, (a, b) in enumerate(CH):
                wait(dve, s_mid, c + 1)
                dve.tensor_tensor(parts[:, a:b, 2 * D:], centred[:, a:b, :], parts[:, a:b, D:2 * D],
                                  ALU.subtract).then_inc(s_parts, 1)

            wait(dve, s_dst, 16 * (edge_dmas + 3))
            dve.tensor_reduce(tile_min[:, :], nat_dst[:, :, :], AX, ALU.min)
            dve.tensor_reduce(tile_max[:, :], nat_dst[:, :, :], AX, ALU.max).then_inc(s_minmax, 1)

            wait(dve, s_minmaxT, 1)
            pairs = lambda t: t.rearrange("b (s t) -> b s t", t=ST)
            dve.tensor_reduce(super_min[:, :], pairs(ps[4][0:EB, 0:P]), AX, ALU.min)
            link(dve.tensor_reduce(super_max[:, :], pairs(ps[4][0:EB, P:2 * P]), AX, ALU.max))
            dve.tensor_copy(super_base[:, :], super_min[:, :]).then_inc(s_base, 1)
            dve.tensor_copy(pairs(base_spread[:, :]), spread(super_min[:, :], ST))
            link(dve.tensor_tensor(super_span[:, :], super_max[:, :], super_min[:, :], ALU.subtract))
            dve.tensor_reduce(span[:, :], super_span[:, :], AX, ALU.max).then_inc(s_spread, 1)

            wait(dve, s_spreadT, 1)
            link(dve.tensor_copy(base_nat[:, :], ps[5][:, 0:EB]))
            dve.tensor_reduce(span_all[:, :], ps[5][0:1, P:P + EB], AX, ALU.max).then_inc(s_flag, 1)

            wait(dve, s_typ, 16 * edge_dmas)
            link(dve.tensor_tensor(nat_b[:, :, :], nat_dst[:, :, :], spread(base_nat[:, :], P), ALU.subtract))
            dve.scalar_tensor_tensor(nat_b[:, :, :].rearrange("q b p -> q (b p)"), nat_typ[:, :, :].rearrange("q b p -> q (b p)"),
                                     float(WIN), nat_b[:, :, :].rearrange("q b p -> q (b p)"), ALU.mult, ALU.add).then_inc(s_key, 1)
            wait(dve, s_add, 1)

            def fast(dve):
                wait(dve, s_base_row, 16)
                wait(dve, s_consts, 1)

                def one_hots(n, b, j, tiles=ST):
                    wait(dve, s_sup, n * SB + j - RING + 1)
                    r = j % RING * ST
                    columns = ps_iota[:, 0:COLS].rearrange("p (o c) -> p o c", o=1).to_broadcast([P, tiles, COLS])
                    dve.tensor_tensor(onehot[:, r:r + tiles, :], columns, spread(key_slot[:, b, j * ST:j * ST + tiles], COLS),
                                      ALU.is_equal).then_inc(s_oh, 1)

                def node_hots(b, pieces):
                    for piece in pieces:
                        lo, hi = PIECES[piece]
                        edges = src_own[:, b, :].rearrange("p (o e) -> p o e", o=1).to_broadcast([P, hi - lo, P])
                        dve.tensor_tensor(node_hot[:, lo:hi, :], edges, spread(ps_nodes[:, lo:hi], P),
                                          ALU.is_equal).then_inc(s_own_hot, 1)

                def add_windows(n, b, windows):
                    _, bases = nc.values_load_multi_w_load_instructions(
                        base_row[0:1, bass.ds(n * SB + windows[0], len(windows))],
                        engines=[dve.engine], min_val=0, max_val=N)
                    wait(dve, s_fl, n + 1)
                    for j, base in zip(windows, bases):
                        wait(dve, s_add, 1 + n * SB + j)
                        here = accT[:, bass.ds(base, WIN)]
                        dve.tensor_tensor(here, here, ps_fl[b][0:D, j * WIN:(j + 1) * WIN], ALU.add).then_inc(s_add, 1)

                def batch(n, b, tiles=BT, fetch=True):
                    supers = -(-tiles // ST)
                    adds = {6: range(4), 7: range(4, SB)} if supers == SB else {supers - 1: range(SB)}
                    wait(dve, s_ks, n + 1)
                    for j in range(supers):
                        one_hots(n, b, j, min(ST, tiles - j * ST))
                        if fetch and j in MADE_AFTER:
                            if j == min(MADE_AFTER):
                                wait(dve, s_own_src[1 - b], 8 * (n + 2 - b) if not isinstance(n, int) else 16 * ((n + 2 - b) // 2))
                            node_hots(1 - b, MADE_AFTER[j])
                        if j in adds and (not isinstance(n, int) or n > 0):
                            add_windows(n - 1, 1 - b, adds[j])

                batch(0, 0)
                with dve.Fori(0, NB // 2 - 1) as i:
                    batch(2 * i + 1, 1)
                    batch(2 * i + 2, 0)
                batch(NB - 2, 1)
                batch(NB - 1, 0, fetch=False)
                batch(NB, 1, LT, fetch=False)
                add_windows(NB, 1, range(LS))

            def general(dve):
                row_of = lambda t: t[:, :, :].rearrange("q b p -> q (b p)")
                wait(dve, s_ix, 1)
                wait(dve, s_keyT, len(key_banks))
                dve.scalar_tensor_tensor(row_of(nat_a), row_of(nat_src), float(R), row_of(nat_typ), ALU.mult, ALU.add)
                dve.tensor_copy(nat_b[:, :, :], nat_dst[:, :, :]).then_inc(s_prep, 1)

                def group(g):
                    for k in range(GT):
                        wait(dve, s_mmT, 2 * (g * GT + k) + 2)
                        wait(dve, s_tw[k], 16 * g)
                        dve.tensor_copy(t_sb[:, k, HALF:], ps[4 + k % 2][:, 0:HALF]).then_inc(s_ev[1], 1)

                group(0)
                with dve.Fori(1, NG) as g:
                    group(g)
                wait(dve, s_iota, 3)
                wait(dve, s_prepE, len(key_banks))

                with dve.Fori(0, GS + 1) as s:
                    dve.tensor_copy(idx_slot[:, 0, 0:GST], row_idx[:, bass.ts(s, GST)]).then_inc(s_gix, 1)
                    with dve.Fori(0, NT) as w:
                        u = s * NT + w
                        nodes = iota_nodes[:, bass.ts(w, P)].rearrange("p (o w) -> p o w", o=1).to_broadcast([P, GST, P])
                        dve.tensor_tensor(gonehot[:, :, :], nodes, spread(key[:, bass.ts(s, GST)], P),
                                          ALU.is_equal).then_inc(s_goh, 1)
                        wait(dve, s_gmm, u + 1)
                        here = accT[:, bass.ts(w, P)]
                        dve.tensor_tensor(here, here, ps[0][0:D, 0:P], ALU.add).then_inc(s_gadd, 1)
                        wait(dve, s_gadd, u + 1)

            fast_or_general(dve, fast, general)
            dve.memset(stat_sum[:, 0:1], 0.0).then_inc(s_acc, 1)

            for g in range(NG):
                wait(dve, s_oT, g + 1)
                tiles = slice(g * GT, (g + 1) * GT)
                dve.tensor_tensor(res[:, tiles, :], ps[g % 4][:, 0:GT * D].rearrange("p (t d) -> p t d", d=D),
                                  x_sb[:, tiles, :], ALU.add).then_inc(s_res, 1)

        @block.tensor
        def _(pe):
            def turn(nat, banks, done):
                for n, (a, b) in enumerate(key_banks):
                    for k in range(a, b):
                        last = pe.transpose(banks(n)[:, (k - a) * P:(k - a + 1) * P], nat[:, k, :], ident[:, :])
                    last.then_inc(done, 1)

            wait(pe, s_id, 2)
            wait(pe, s_idx, 1)
            turn(nat_a, lambda n: ps[n], s_idxT)
            wait(pe, s_minmax, 1)
            pe.transpose(ps[4][0:EB, 0:P], tile_min[:, :], ident[:, :])
            pe.transpose(ps[4][0:EB, P:2 * P], tile_max[:, :], ident[:, :]).then_inc(s_minmaxT, 1)
            wait(pe, s_spread, 1)
            pe.transpose(ps[5][:, 0:EB], base_spread[:, :], ident[0:EB, 0:EB])
            pe.transpose(ps[5][0:1, P:P + EB], span[:, :], ident[0:EB, 0:EB]).then_inc(s_spreadT, 1)
            wait(pe, s_key, 1)
            wait(pe, s_idxE, len(key_banks))
            turn(nat_b, lambda n: ps[n], s_keyT)

            def fast(pe):
                wait(pe, s_w, 64)
                wait(pe, s_keyE, len(key_banks))

                def fetch_own(n, pieces):
                    for piece in pieces:
                        wait(pe, s_own_hot, len(PIECES) * n + piece + 1)
                        if piece == 0:
                            wait(pe, s_own, n)
                        for t in range(*PIECES[piece]):
                            last = pe.matmul(ps_own[:, 0:ROW], node_hot[:, t, :], parts[:, t, :], start=t == 0, stop=t == NT - 1)
                    if pieces[-1] == len(PIECES) - 1:
                        last.then_inc(s_own_sum, 1)

                def sum_super(n, b, j, tiles=ST):
                    q, u = n * (SB // HMB) + j // HMB, n * (SB // LOB) + j // LOB
                    hm = ps_hm[j // HMB % 2][:, j % HMB * COLS:(j % HMB + 1) * COLS]
                    lo = ps_lo[j // LOB % 2][:, j % LOB * COLS // 2:(j % LOB + 1) * COLS // 2]
                    if j % HMB == 0:
                        wait(pe, s_eh, q - 1)
                    if j % LOB == 0:
                        wait(pe, s_el, u - 1)
                    wait(pe, s_oh, n * SB + j + 1)
                    for t in range(tiles):
                        k = j * ST + t
                        rows = EREM if tiles < ST else P
                        if k == OWN and not (isinstance(n, int) and n == 0):
                            wait(pe, s_own, n)
                        else:
                            wait(pe, s_g[b][k], 16 * (n // 2 + 1) if isinstance(n, int) else 8 * n + (16 - 8 * b))
                        start, stop = t == 0, t == tiles - 1
                        hot = onehot[0:rows, j % RING * ST + t, :]
                        pe.matmul(hm, msg[0:rows, b, k, 0:P], hot, start=start, stop=stop)
                        for half in range(2):
                            last = pe.matmul(lo[half * D:(half + 1) * D, :], msg[0:rows, b, k, P:ROW],
                                             hot[:, half * COLS // 2:(half + 1) * COLS // 2], start=start, stop=stop)
                    last.then_inc(s_sup, 1)

                def weigh(n, b, supers=SB):
                    wait(pe, s_eh, n * (SB // HMB) + -(-supers // HMB))
                    wait(pe, s_el, n * (SB // LOB) + -(-supers // LOB))
                    wait(pe, s_add, 1 + (n - 1) * SB)
                    fl = ps_fl[b][0:D, 0:supers * WIN]
                    for r in range(R):
                        pe.matmul(fl, w_hm[:, r, :], agg_hm[:, b, 0:supers, r * WIN:(r + 1) * WIN], start=r == 0, stop=False)
                    for r in range(R // 2):
                        last = pe.matmul(fl, w_lo[:, r, :], agg_lo[:, b, 0:supers, r * WIN:(r + 1) * WIN],
                                         start=False, stop=r == R // 2 - 1)
                    last.then_inc(s_fl, 1)

                def batch(n, b, tiles=BT, fetch=True):
                    for j in range(-(-tiles // ST)):
                        sum_super(n, b, j, min(ST, tiles - j * ST))
                        if fetch and j in USED_AFTER:
                            fetch_own(n, USED_AFTER[j])
                        if j == 1 and (not isinstance(n, int) or n > 0):
                            weigh(n - 1, 1 - b)

                batch(0, 0)
                batch(1, 1)
                batch(2, 0)
                with pe.Fori(1, NB // 2 - 1) as i:
                    batch(2 * i + 1, 1)
                    batch(2 * i + 2, 0)
                batch(NB - 2, 1)
                batch(NB - 1, 0, fetch=False)
                batch(NB, 1, LT, fetch=False)
                weigh(NB, 1, LS)

            def general(pe):
                wait(pe, s_keyE, len(key_banks))
                wait(pe, s_prep, 1)
                for n, (a, b) in enumerate(key_banks):
                    if n == 3:
                        wait(pe, s_prepE, 1)
                    for nat, bank in ((nat_a, ps[n]), (nat_b, ps[4 + n % 3])):
                        for k in range(a, b):
                            last = pe.transpose(bank[:, (k - a) * P:(k - a + 1) * P], nat[:, k, :], ident[:, :])
                    last.then_inc(s_prepT, 1)
                wait(pe, s_prepE, len(key_banks))
                wait(pe, s_w, 64)

                def group(g):
                    hold(pe, s_gh, g + 1)
                    hold(pe, s_hT, 2 * g)
                    for part, (a, b) in enumerate(halves):
                        for k in range(a, b):
                            last = pe.transpose(ps[part][0:D, (k - a) * P:(k - a + 1) * P], gh[:, k, :], ident[:, :])
                        last.then_inc(s_hp, 1)
                    for k in range(GT):
                        if k in (0, 4):
                            hold(pe, s_hT, 2 * g + (1 if k == 0 else 2))
                        n = g * GT + k
                        prev = n - 1 if k > 1 else n - 2 if k == 1 else n
                        for half in range(2):
                            wait(pe, s_ev[half], prev)
                            pe.matmul(ps[2 + 2 * half + k % 2][:, 0:HALF], ghT[:, k, :],
                                      w_hm[0:D, half * R // 2:(half + 1) * R // 2, :].rearrange("i r o -> i (r o)"),
                                      start=True, stop=True).then_inc(s_mmT, 1)

                group(0)
                with pe.Fori(1, NG) as g:
                    group(g)

                def supertile(s, tiles=GST):
                    for k in range(tiles):
                        hold(pe, s_gg[k], 16 * (s + 1))
                    with pe.Fori(0, NT) as w:
                        wait(pe, s_goh, s * NT + w + 1)
                        for k in range(tiles):
                            rows = last_rows(k, tiles, GST)
                            last = pe.matmul(ps[0][0:D, 0:P], gmsg[0:rows, k, :], gonehot[0:rows, k, :],
                                             start=(k == 0), stop=(k == tiles - 1))
                        last.then_inc(s_gmm, 1)

                with pe.Fori(0, GS) as s:
                    supertile(s)
                supertile(GS, GTAIL)

            fast_or_general(pe, fast, general)

            wait(pe, s_acc, 1)
            for g in range(NG):
                wait(pe, s_res, g - 3)
                for k in range(GT):
                    t = g * GT + k
                    last = pe.transpose(ps[g % 4][:, k * D:(k + 1) * D], accT[:, t:NT * P:NT], ident[0:D, 0:D])
                last.then_inc(s_oT, 1)


def kernel(x, src, dst, edge_type_16, L0_gnn_weight):
    from concourse import bacc
    from concourse.bass_utils import run_bass_kernel_spmd

    given = {"x": x, "src": src, "dst": dst, "edge_type": edge_type_16, "weight": L0_gnn_weight}
    arrays = {name: np.ascontiguousarray(a) for name, a in given.items()}
    nc = bacc.Bacc("TRN2", target_bir_lowering=False, num_devices=1)
    aps = [nc.dram_tensor(name, a.shape, mybir.dt.from_np(a.dtype), kind="ExternalInput").ap()
           for name, a in arrays.items()]
    out = nc.dram_tensor("out", arrays["x"].shape, F32, kind="ExternalOutput").ap()
    gnn_program(nc, *aps, out)
    run = run_bass_kernel_spmd(nc, [arrays], core_ids=[0])
    return run.results[0]["out"]
```
